# Optimizing a Trainium2 kernel written in Bass

```python
import numpy as np
import jax
import jax.numpy as jnp

def _softmax(x, axis=-1):
    return jax.nn.softmax(x, axis=axis)

def _gelu(x):
    return jax.nn.gelu(x, approximate=True)

def _silu(x):
    return jax.nn.silu(x)

def _sigmoid(x):
    return jax.nn.sigmoid(x)

def _layernorm(x, axis=-1, eps=1e-05):
    m = jnp.mean(x, axis=axis, keepdims=True)
    v = jnp.var(x, axis=axis, keepdims=True)
    return (x - m) / jnp.sqrt(v + eps)

def _scatter_add(tgt, idx, src, axis=0):
    return tgt.at[idx].add(src)

def _segment_sum(src, seg, n):
    return jax.ops.segment_sum(src, seg, n)
kernel_name = 'mk_audio_tower_d1_tok_audfeat512_r4_019199'

def setup_inputs(seed: int=0):
    np.random.seed(seed)
    _w = jnp.asarray

    def _rec_inputs():
        import jax
        import jax.numpy as jnp
        _rk = jax.random.key(seed)
        x = -0.000392918 + 0.999932 * jax.random.normal(jax.random.fold_in(_rk, 1), (128, 125, 128), jnp.float32)
        return x
    x = _rec_inputs()

    def _L0_tok_setup():
        import jax, jax.numpy as jnp
        import numpy as np
        B, T, D, H = (8, 1024, 128, 128)

        def _linear_params(key, d_in, d_out):
            k1, k2 = jax.random.split(key)
            bound = 1.0 / np.sqrt(d_in)
            W = jax.random.uniform(k1, (d_in, d_out), jnp.float32, -bound, bound)
            b = jax.random.uniform(k2, (d_out,), jnp.float32, -bound, bound)
            return (W, b)

        def _log_g(z):
            return jnp.where(z >= 0, jnp.log(jax.nn.relu(z) + 0.5), -jax.nn.softplus(-z))
        key = jax.random.key(seed)
        kx, kf, ki, kh = jax.random.split(key, 4)
        x = jax.random.normal(kx, (B, T, D), dtype=jnp.float32)
        Wf, bf = _linear_params(kf, D, H)
        Wi, bi = _linear_params(ki, D, H)
        Wh, bh = _linear_params(kh, D, H)
        return {'x': x, 'Wf': Wf, 'bf': bf, 'Wi': Wi, 'bi': bi, 'Wh': Wh, 'bh': bh}
    _L0_tok_all = _L0_tok_setup()
    _L0_tok_in = {k: v for k, v in _L0_tok_all.items() if k in ('Wf', 'bf', 'Wi', 'bi', 'Wh', 'bh')}
    del _L0_tok_all

    def _L0_attn_setup():
        import jax, jax.numpy as jnp
        import numpy as np
        B, S, D, H = (4, 512, 128, 8)
        KD = D // H
        FFN = 4 * D

        def _ln(x, g, b, eps):
            mu = x.mean(-1, keepdims=True)
            var = ((x - mu) ** 2).mean(-1, keepdims=True)
            return (x - mu) / jnp.sqrt(var + eps) * g + b
        key = jax.random.key(seed)
        ks = jax.random.split(key, 8)

        def lin(k, o, i, scale=0.02):
            k1, k2 = jax.random.split(k)
            return (jax.random.normal(k1, (o, i), jnp.float32) * scale, jax.random.normal(k2, (o,), jnp.float32) * scale)
        wq, bq = lin(ks[0], D, D)
        wk, bk = lin(ks[1], D, D)
        wv, bv = lin(ks[2], D, D)
        wg, bg = lin(ks[3], D, D)
        wo, bo = lin(ks[4], D, D)
        fc1_w, fc1_b = lin(ks[5], FFN, D)
        fc2_w, fc2_b = lin(ks[6], D, FFN)
        return {'src': jax.random.normal(ks[7], (B, S, D), jnp.float32), 'mask': jnp.zeros((S, S), jnp.bool_), 'padding_mask': jnp.zeros((B, S), jnp.bool_), 'wq': wq, 'bq': bq, 'wk': wk, 'bk': bk, 'wv': wv, 'bv': bv, 'wg': wg, 'bg': bg, 'wo': wo, 'bo': bo, 'fc1_w': fc1_w, 'fc1_b': fc1_b, 'fc2_w': fc2_w, 'fc2_b': fc2_b, 'ln_ffn_g': jnp.ones((FFN,), jnp.float32), 'ln_ffn_b': jnp.zeros((FFN,), jnp.float32), 'n0_g': jnp.ones((D,), jnp.float32), 'n0_b': jnp.zeros((D,), jnp.float32), 'n1_g': jnp.ones((D,), jnp.float32), 'n1_b': jnp.zeros((D,), jnp.float32)}
    _L0_attn_all = _L0_attn_setup()
    _L0_attn_in = {k: v for k, v in _L0_attn_all.items() if k in ('mask', 'padding_mask', 'wq', 'bq', 'wk', 'bk', 'wv', 'bv', 'wg', 'bg', 'wo', 'bo', 'fc1_w', 'fc1_b', 'fc2_w', 'fc2_b', 'ln_ffn_g', 'ln_ffn_b', 'n0_g', 'n0_b', 'n1_g', 'n1_b')}
    del _L0_attn_all

    def _L0_ffn_setup():
        import jax, jax.numpy as jnp
        import numpy as np
        TOP_K = 6
        CAP_FACTOR = 2.0
        key = jax.random.key(seed)
        ks = jax.random.split(key, 9)
        B, S, D, F, E, SH = (4, 512, 128, 64, 64, 2)
        return {'x': jax.random.normal(ks[0], (B, S, D), jnp.float32), 'router_w': jax.random.normal(ks[1], (E, D), jnp.float32) * 0.02, 'bias': jnp.zeros((E,), jnp.float32), 'shared_w_gate': jax.random.normal(ks[2], (SH, F, D), jnp.float32) * 0.02, 'shared_w_up': jax.random.normal(ks[3], (SH, F, D), jnp.float32) * 0.02, 'shared_w_down': jax.random.normal(ks[4], (SH, D, F), jnp.float32) * 0.02, 'w_gate': jax.random.normal(ks[5], (E, F, D), jnp.float32) * 0.02, 'w_up': jax.random.normal(ks[6], (E, F, D), jnp.float32) * 0.02, 'w_down': jax.random.normal(ks[7], (E, D, F), jnp.float32) * 0.02}
    _L0_ffn_all = _L0_ffn_setup()
    _L0_ffn_in = {k: v for k, v in _L0_ffn_all.items() if k in ('router_w', 'bias', 'shared_w_gate', 'shared_w_up', 'shared_w_down', 'w_gate', 'w_up', 'w_down')}
    del _L0_ffn_all
    return {'x': x, 'L0_tok_Wf': _L0_tok_in['Wf'], 'L0_tok_bf': _L0_tok_in['bf'], 'L0_tok_Wi': _L0_tok_in['Wi'], 'L0_tok_bi': _L0_tok_in['bi'], 'L0_tok_Wh': _L0_tok_in['Wh'], 'L0_tok_bh': _L0_tok_in['bh'], 'L0_attn_mask': _L0_attn_in['mask'], 'L0_attn_padding_mask': _L0_attn_in['padding_mask'], 'L0_attn_wq': _L0_attn_in['wq'], 'L0_attn_bq': _L0_attn_in['bq'], 'L0_attn_wk': _L0_attn_in['wk'], 'L0_attn_bk': _L0_attn_in['bk'], 'L0_attn_wv': _L0_attn_in['wv'], 'L0_attn_bv': _L0_attn_in['bv'], 'L0_attn_wg': _L0_attn_in['wg'], 'L0_attn_bg': _L0_attn_in['bg'], 'L0_attn_wo': _L0_attn_in['wo'], 'L0_attn_bo': _L0_attn_in['bo'], 'L0_attn_fc1_w': _L0_attn_in['fc1_w'], 'L0_attn_fc1_b': _L0_attn_in['fc1_b'], 'L0_attn_fc2_w': _L0_attn_in['fc2_w'], 'L0_attn_fc2_b': _L0_attn_in['fc2_b'], 'L0_attn_ln_ffn_g': _L0_attn_in['ln_ffn_g'], 'L0_attn_ln_ffn_b': _L0_attn_in['ln_ffn_b'], 'L0_attn_n0_g': _L0_attn_in['n0_g'], 'L0_attn_n0_b': _L0_attn_in['n0_b'], 'L0_attn_n1_g': _L0_attn_in['n1_g'], 'L0_attn_n1_b': _L0_attn_in['n1_b'], 'L0_ffn_router_w': _L0_ffn_in['router_w'], 'L0_ffn_bias': _L0_ffn_in['bias'], 'L0_ffn_shared_w_gate': _L0_ffn_in['shared_w_gate'], 'L0_ffn_shared_w_up': _L0_ffn_in['shared_w_up'], 'L0_ffn_shared_w_down': _L0_ffn_in['shared_w_down'], 'L0_ffn_w_gate': _L0_ffn_in['w_gate'], 'L0_ffn_w_up': _L0_ffn_in['w_up'], 'L0_ffn_w_down': _L0_ffn_in['w_down']}

def reference(x, L0_tok_Wf, L0_tok_bf, L0_tok_Wi, L0_tok_bi, L0_tok_Wh, L0_tok_bh, L0_attn_mask, L0_attn_padding_mask, L0_attn_wq, L0_attn_bq, L0_attn_wk, L0_attn_bk, L0_attn_wv, L0_attn_bv, L0_attn_wg, L0_attn_bg, L0_attn_wo, L0_attn_bo, L0_attn_fc1_w, L0_attn_fc1_b, L0_attn_fc2_w, L0_attn_fc2_b, L0_attn_ln_ffn_g, L0_attn_ln_ffn_b, L0_attn_n0_g, L0_attn_n0_b, L0_attn_n1_g, L0_attn_n1_b, L0_ffn_router_w, L0_ffn_bias, L0_ffn_shared_w_gate, L0_ffn_shared_w_up, L0_ffn_shared_w_down, L0_ffn_w_gate, L0_ffn_w_up, L0_ffn_w_down):
    import jax
    import jax.numpy as jnp

    def _L0_tok_ref(x, Wf, bf, Wi, bi, Wh, bh):
        import jax, jax.numpy as jnp
        import numpy as np
        B, T, D, H = (8, 1024, 128, 128)

        def _linear_params(key, d_in, d_out):
            k1, k2 = jax.random.split(key)
            bound = 1.0 / np.sqrt(d_in)
            W = jax.random.uniform(k1, (d_in, d_out), jnp.float32, -bound, bound)
            b = jax.random.uniform(k2, (d_out,), jnp.float32, -bound, bound)
            return (W, b)

        def _log_g(z):
            return jnp.where(z >= 0, jnp.log(jax.nn.relu(z) + 0.5), -jax.nn.softplus(-z))
        b, t, h = (x.shape[0], x.shape[1], Wf.shape[1])
        zf = x @ Wf + bf
        zi = x @ Wi + bi
        zh = x @ Wh + bh
        diff = jax.nn.softplus(-zf) - jax.nn.softplus(-zi)
        log_f = -jax.nn.softplus(diff)
        log_i = -jax.nn.softplus(-diff)
        log_h0 = jnp.full((b, 1, h), jnp.log(jnp.float32(0.5)), dtype=x.dtype)
        log_tilde_h = _log_g(zh)
        log_val = jnp.concatenate([log_h0, log_i + log_tilde_h], axis=1)
        a_star = jnp.concatenate([jnp.zeros((b, 1, h), dtype=x.dtype), log_f], axis=1)
        log_h = a_star + jax.lax.cumlogsumexp(log_val - a_star, axis=1)
        return jnp.exp(log_h)

    def _L0_attn_ref(src, mask, padding_mask, wq, bq, wk, bk, wv, bv, wg, bg, wo, bo, fc1_w, fc1_b, fc2_w, fc2_b, ln_ffn_g, ln_ffn_b, n0_g, n0_b, n1_g, n1_b):
        import jax, jax.numpy as jnp
        import numpy as np
        B, S, D, H = (4, 512, 128, 8)
        KD = D // H
        FFN = 4 * D

        def _ln(x, g, b, eps):
            mu = x.mean(-1, keepdims=True)
            var = ((x - mu) ** 2).mean(-1, keepdims=True)
            return (x - mu) / jnp.sqrt(var + eps) * g + b
        b, s, d = src.shape
        idx = jnp.arange(s)
        diff = (idx[:, None] - idx[None, :]).astype(src.dtype)
        decay = jnp.log(1.0 - 2.0 ** (-5.0 - jnp.arange(H, dtype=src.dtype)))
        dm = jnp.where(diff[None] >= 0, jnp.exp(diff[None] * decay[:, None, None]), 0.0)
        dm = dm / jnp.sqrt(dm.sum(-1, keepdims=True))
        q = (src @ wq.T + bq).reshape(b, s, H, KD).transpose(0, 2, 1, 3)
        k = ((src @ wk.T + bk) * KD ** (-0.5)).reshape(b, s, H, KD).transpose(0, 2, 1, 3)
        v = src @ wv.T + bv
        g = src @ wg.T + bg
        qk = jnp.einsum('bhid,bhjd->bhij', q, k) + dm[None]
        den = jnp.maximum(jnp.abs(jax.lax.stop_gradient(qk).sum(-1, keepdims=True)), 1.0)
        qk = qk / den
        vr = v.reshape(b, s, H, KD).transpose(0, 2, 1, 3)
        o = jnp.einsum('bhij,bhjd->bhid', qk, vr).transpose(0, 2, 1, 3)
        mu = o.mean(-1, keepdims=True)
        o = (o - mu) / jnp.sqrt(((o - mu) ** 2).mean(-1, keepdims=True) + 1e-06)
        o = jax.nn.silu(g) * o.reshape(b, s, d)
        o = o @ wo.T + bo
        x = _ln(src + o, n0_g, n0_b, 1e-05)
        h = jax.nn.gelu(x @ fc1_w.T + fc1_b, approximate=False)
        h = _ln(h, ln_ffn_g, ln_ffn_b, 1e-06)
        h = h @ fc2_w.T + fc2_b
        return _ln(x + h, n1_g, n1_b, 1e-05)

    def _L0_ffn_ref(x, router_w, bias, shared_w_gate, shared_w_up, shared_w_down, w_gate, w_up, w_down):
        import jax, jax.numpy as jnp
        import numpy as np
        TOP_K = 6
        CAP_FACTOR = 2.0
        B, S, D = x.shape
        E = router_w.shape[0]
        K = TOP_K
        N = B * S
        C = max(1, int(N * K * CAP_FACTOR / E))
        router_logits = jnp.einsum('bsd,ed->bse', x, router_w) + bias
        hg = jnp.einsum('bsd,efd->bsef', x, shared_w_gate)
        hu = jnp.einsum('bsd,efd->bsef', x, shared_w_up)
        shared_out = jnp.einsum('bsef,edf->bsd', jax.nn.silu(hg) * hu, shared_w_down)
        shared_out = shared_out / shared_w_gate.shape[0]
        router_probs = jax.nn.softmax(router_logits, axis=-1)
        topk_p, topk_i = jax.lax.top_k(router_probs, K)
        topk_p = topk_p / (jnp.sum(topk_p, axis=-1, keepdims=True) + 1e-09)
        x_flat = x.reshape(N, D)
        flat_e = topk_i.reshape(-1)
        flat_g = topk_p.reshape(-1)
        token_ids = jnp.repeat(jnp.arange(N), K)
        order = jnp.argsort(flat_e)
        se = flat_e[order]
        st = token_ids[order]
        sg = flat_g[order]
        M = se.shape[0]
        pos = jnp.arange(M)
        is_first = jnp.concatenate([jnp.ones((1,), bool), se[1:] != se[:-1]])
        group_starts = jax.lax.cummax(pos * is_first.astype(pos.dtype))
        slot = pos - group_starts
        valid = slot < C
        safe_slot = jnp.where(valid, slot, C)
        expert_in = jnp.zeros((E, C + 1, D), x.dtype).at[se, safe_slot].set(x_flat[st])
        expert_gate = jnp.zeros((E, C + 1), x.dtype).at[se, safe_slot].set(sg)
        expert_tok = jnp.full((E, C + 1), N, jnp.int32).at[se, safe_slot].set(st.astype(jnp.int32))
        expert_mask = jnp.zeros((E, C + 1), bool).at[se, safe_slot].set(valid)
        expert_in = expert_in[:, :C]
        expert_gate = expert_gate[:, :C]
        expert_tok = expert_tok[:, :C]
        expert_mask = expert_mask[:, :C]
        hg = jnp.einsum('ecd,efd->ecf', expert_in, w_gate)
        hu = jnp.einsum('ecd,efd->ecf', expert_in, w_up)
        expert_out = jnp.einsum('ecf,edf->ecd', jax.nn.silu(hg) * hu, w_down)
        fm = expert_mask.reshape(-1)
        dst = jnp.where(fm, expert_tok.reshape(-1), N)
        fg = jnp.where(fm, expert_gate.reshape(-1), jnp.zeros((), x.dtype))
        sparse = jax.ops.segment_sum(fg[:, None] * expert_out.reshape(-1, D), dst, num_segments=N + 1)[:N]
        return shared_out + sparse.reshape(B, S, D)
    h = _L0_tok_ref(x, L0_tok_Wf, L0_tok_bf, L0_tok_Wi, L0_tok_bi, L0_tok_Wh, L0_tok_bh)
    h = h + _L0_attn_ref(_layernorm(h, axis=-1), L0_attn_mask, L0_attn_padding_mask, L0_attn_wq, L0_attn_bq, L0_attn_wk, L0_attn_bk, L0_attn_wv, L0_attn_bv, L0_attn_wg, L0_attn_bg, L0_attn_wo, L0_attn_bo, L0_attn_fc1_w, L0_attn_fc1_b, L0_attn_fc2_w, L0_attn_fc2_b, L0_attn_ln_ffn_g, L0_attn_ln_ffn_b, L0_attn_n0_g, L0_attn_n0_b, L0_attn_n1_g, L0_attn_n1_b)
    h = h + _L0_ffn_ref(_layernorm(h, axis=-1), L0_ffn_router_w, L0_ffn_bias, L0_ffn_shared_w_gate, L0_ffn_shared_w_up, L0_ffn_shared_w_down, L0_ffn_w_gate, L0_ffn_w_up, L0_ffn_w_down)
    return h

_drawn_inputs = setup_inputs


def setup_inputs(seed=0):
    import zlib

    import numpy as np

    out = dict(_drawn_inputs(seed))
    spreads = {'L0_attn_ln_ffn_g': (1.0, 0.6),
     'L0_attn_ln_ffn_b': (0.0, 0.8),
     'L0_attn_n0_g': (1.0, 0.6),
     'L0_attn_n0_b': (0.0, 0.8),
     'L0_attn_n1_g': (1.0, 0.6),
     'L0_attn_n1_b': (0.0, 0.8),
     'L0_ffn_bias': (0.0, 2.0)}
    factors = {'L0_tok_bf': 3.116,
     'L0_tok_bi': 4.376,
     'L0_attn_wq': 8.0,
     'L0_attn_bq': 42.728,
     'L0_attn_wk': 8.0,
     'L0_attn_bk': 44.983,
     'L0_attn_wv': 8.0,
     'L0_attn_bv': 57.027,
     'L0_attn_wg': 8.0,
     'L0_attn_bg': 46.292,
     'L0_attn_wo': 8.0,
     'L0_attn_bo': 53.181,
     'L0_attn_fc1_w': 3.63,
     'L0_attn_fc1_b': 40.557,
     'L0_attn_fc2_w': 3.531,
     'L0_attn_fc2_b': 64.0,
     'L0_ffn_router_w': 8.0,
     'L0_ffn_shared_w_gate': 8.0,
     'L0_ffn_shared_w_up': 8.0,
     'L0_ffn_shared_w_down': 8.0,
     'L0_ffn_w_gate': 8.0,
     'L0_ffn_w_up': 8.0,
     'L0_ffn_w_down': 8.0}
    for name, (base, spread) in spreads.items():
        noise = np.random.default_rng([zlib.crc32(name.encode()), seed]).standard_normal(out[name].shape)
        drawn = base * np.exp(spread * noise) if base else spread * noise
        out[name] = jnp.asarray(drawn.astype(out[name].dtype))
    for name, factor in factors.items():
        out[name] = (out[name] * factor).astype(out[name].dtype)
    return out
```

```python
import concourse.bass as bass
from concourse import mybir
from contextlib import ExitStack

SEQS, T_IN, D = 128, 125, 128
T = T_IN + 1
GS = 4
GROUPS = SEQS // GS
N = GS * T
HEADS, KD = 8, 16
FC = 4
E, F = 64, 64
PAIRS = E // 2 + 1
SHARED = PAIRS - 1
TOP_K = 6
CAPACITY = SEQS * T * TOP_K * 2 // E
LAG = 2
BIG = 3.0e38

A_PE = ["zf_zi", "zh", "center", "var", "spread", "kv", "qg", "outer", "mix", "turn", "wo"]
A_ACT = ["zf", "zi", "zh", "abs", "exps", "c", "sq", "q", "g", "osq"]
A_DVE = ["mf", "mi", "mh", "n2", "d", "e", "m", "nd", "rd", "mr", "dm", "em",
         "ti", "tf", "pp", "pn", "a", "b", "den", "pd", "r1", "r2", "mv1", "mv2", "val", "s", "h1", "h2", "h3", "h",
         "ve", "src", "kv", "bd", "bds", "mu", "oc", "den1", "den2", "den3", "den4", "ovar", "ove", "on", "og", "r"]
A_POOL = ["rs", "ors"]
B_PE = ["center0", "var0", "spread0", "fc1_0", "fc1_1", "fc1_2", "fc1_3", "mean", "var1a", "var1b", "spread1", "fc2",
        "center2", "var2", "spread2", "center3", "var3", "spread3", "router", "rank", "turn"]
B_ACT = ["c0", "sq0", "hb", "hp0", "hp1", "hp2", "hp3", "gelu", "fsq0", "fsq1", "fsq2", "fsq3", "rsb",
         "c2", "sq2", "c3", "sq3", "xh", "exp"]
B_DVE = ["ve0", "t0", "x1", "hs0", "hs1", "hs2", "c_0", "c_1", "c_2", "c_3", "ve1", "r2a", "r2",
         "ve2", "y", "h1", "ve3", "xf", "lg", "top", "big", "match", "mask", "shift",
         "z", "em", "sum", "keep", "nrun", "tot", "inv", "gk", "gate", "gt_hi", "gt_lo"]
B_POOL = ["rs0", "rs1", "rs2", "rs3", "xl"]


def did(steps, step, g):
    return g * len(steps) + steps.index(step) + 1


def from_group(g, n):
    return g >= n if isinstance(g, int) else True


def audio_tower_kernel(nc, x, w, out):
    fp32, f32r = mybir.dt.float32, mybir.dt.float32r
    bf16, fp16 = mybir.dt.bfloat16, mybir.dt.float16
    ALU, ACT = mybir.AluOpType, mybir.ActivationFunctionType
    AX = mybir.AxisListType.X

    ctx = ExitStack()
    with ctx:
        def sb(name, shape, dt=fp32):
            return ctx.enter_context(nc.sbuf_tensor(name, shape, dt))

        def bank(name):
            return ctx.enter_context(nc.psum_tensor(name, [128, 512], fp32))

        def sem(name):
            return ctx.enter_context(nc.semaphore(name))

        whi = sb("whi", [128, 3, PAIRS * 128], f32r)
        wlo = sb("wlo", [128, 3, PAIRS * 128], f32r)
        pick = sb("pick", [128, E * F], fp16)
        wtok = sb("wtok", [D, 3, D])
        wqgo = sb("wqgo", [D, 3, D])
        wkv = sb("wkv", [D, 2 * D])
        wfc1 = sb("wfc1", [D, FC * D])
        wfc2 = sb("wfc2", [D, FC, D])
        wrt = sb("wrt", [D, E])
        cmat = sb("cmat", [D, D])
        jmat = sb("jmat", [D, D])
        nth = sb("nth", [D, 2])
        ident = sb("ident", [T, T])
        dmt = sb("dmt", [T, HEADS, T])
        dsum = sb("dsum", [T, HEADS])
        bdm = sb("bdm", [D, D])
        hm = sb("hm", [D, HEADS])
        keepm = sb("keepm", [D, N])
        before = sb("before", [T, T], bf16)
        all1 = sb("all1", [T, T], bf16)
        ones = sb("ones", [T, 1])
        mhalf = sb("mhalf", [T, GS * HEADS])
        bkv = sb("bkv", [T, 2 * D])
        brt = sb("brt", [T, E])
        cols = sb("cols", [D, 11])
        bfc1 = sb("bfc1", [D, FC])
        lng = sb("lng", [D, FC])
        lnb = sb("lnb", [D, FC])
        cb = sb("cb", [D, 1])
        col = {n: cols[:, i:i + 1] for i, n in enumerate(
            ["bf", "bi", "bh", "bq", "bg", "bo", "n0_g", "n0_b", "n1_g", "n1_b", "fc2_b"])}

        xin = sb("xin", [D, GS * T_IN])
        ar = sb("ar", [128, 8, 512])
        e_t = sb("e_t", [D, N])
        step_t = sb("step_t", [D, N])
        val_t = sb("val_t", [D, N])
        h0 = sb("h0", [D, N])
        bds = sb("bds", [D, GS * HEADS])
        a_small = sb("a_small", [T, 6, GS * HEADS])
        r_t = sb("r_t", [D, N])
        ff = sb("ff", [128, FC, 512])
        b_c = sb("b_c", [D, N])
        b_sq = sb("b_sq", [D, 2, N])
        b_x1 = sb("b_x1", [D, N])
        b_mix = sb("b_mix", [D, N])
        hb = sb("hb", [D, N])
        b_small = sb("b_small", [T, 8, 8])
        lg = sb("lg", [T, GS, E + 2])
        top = sb("top", [T, GS, 8])
        carrier = sb("carrier", [T, 2])
        nrun = sb("nrun", [T, E])
        mask = sb("mask", [T, GS, E], bf16)
        xh = sb("xh", [D, 2, N], f32r)
        xl = sb("xl", [D, 2, N], f32r)
        h1 = sb("h1", [D, 2, N])
        gt = sb("gt", [128, N], fp16)
        s_t = sb("s_t", [128, 2, N])
        t_t = sb("t_t", [128, N])
        h_t = sb("h_t", [128, 2, N])
        hh = sb("hh", [128, 2, N], f32r)
        hl = sb("hl", [128, 2, N], f32r)

        PG = [bank("PG0"), bank("PG1")]
        PU, PB, ACC = bank("PU"), bank("PB"), bank("ACC")
        FA = [bank("FA0"), bank("FA1")]
        FB = bank("FB")

        consts_in = sem("consts_in")
        stage_in = [sem(f"stage_in{i}") for i in range(FC)]
        setup_act, setup_dve, setup_pool, setup_pe = sem("setup_act"), sem("setup_dve"), sem("setup_pool"), sem("setup_pe")
        x_in, out_done = sem("x_in"), sem("out_done")
        a_pe, a_act, a_dve, a_pool = sem("a_pe"), sem("a_act"), sem("a_dve"), sem("a_pool")
        b_pe, b_act, b_dve, b_pool = sem("b_pe"), sem("b_act"), sem("b_dve"), sem("b_pool")
        gate_done, up_done, spread_done, down_done = sem("gate_done"), sem("up_done"), sem("spread_done"), sem("down_done")
        silu_done, prod_done, h_done = sem("silu_done"), sem("prod_done"), sem("h_done")
        hh_done, hl_done, out_ready = sem("hh_done"), sem("hl_done"), sem("out_ready")

        block = ctx.enter_context(nc.Block())

        def seqs(t, lo=0):
            return t.rearrange("p (s t) -> p s t", t=T)[:, :, lo:T]

        tile = [ar[:, i, 0:N] for i in range(8)]
        zv = [FA[0][:, 0:GS * T_IN], FA[1][:, 0:GS * T_IN]]
        zs = [v.rearrange("p (s t) -> p s t", t=T_IN) for v in zv]
        body = lambda t: seqs(t, 1)
        kv = ar[0:T, 3:5, :].rearrange("p a (s c) -> p (a s) c", c=2 * D)
        bdv = ar[:, 5, :].rearrange("p (s c) -> p s c", c=D)
        oc = ar[0:T, 0, :]
        osq = ar[0:T, 1, :]
        heads = lambda t: t.rearrange("p (g k) -> p g k", k=KD)
        over_heads = lambda t: t.unsqueeze(2).to_broadcast([T, GS * HEADS, KD])
        ff_tile = [ff[:, j, 0:N] for j in range(FC)]
        matched = ff[0:T, 0, 0:GS * (E + 2)].rearrange("p (s e) -> p s e", e=E + 2)
        ee = ff[0:T, 1, 0:GS * E].rearrange("p (s e) -> p s e", e=E)
        gk = ff[0:T, 2, 0:GS * E].rearrange("p (s e) -> p s e", e=E)
        g2 = ff[0:T, 3, :].rearrange("p (s e) -> p s e", e=2 * E)
        per_seq = lambda t: t.unsqueeze(2).to_broadcast([T, GS, E])
        router_out = FB[0:T, 0:GS * E].rearrange("p (s e) -> p s e", e=E)

        chunks = [(k, c, min(512, PAIRS * 128 - c)) for k in range(3) for c in range(0, PAIRS * 128, 512)]
        const_loads = [
            (wtok[:, 0, :], w["wf"]), (wtok[:, 1, :], w["wi"]), (wtok[:, 2, :], w["wh"]),
            (cols[:, 0:1], w["bf"]), (cols[:, 1:2], w["bi"]), (cols[:, 2:3], w["bh"]),
            (keepm[:, :], w["keepm"]), (cmat[:, :], w["cmat"]), (nth[:, :], w["nth"]), (ident[:, :], w["ident"]),
            (wkv[:, 0:D], w["wk"]), (wkv[:, D:2 * D], w["wv"]),
            (bkv[:, 0:D], w["bk"].to_broadcast([T, D])), (bkv[:, D:2 * D], w["bv"].to_broadcast([T, D])),
            (wqgo[:, 0, :], w["wq"]), (wqgo[:, 1, :], w["wg"]), (wqgo[:, 2, :], w["wo"]),
            (cols[:, 3:4], w["bq"]), (cols[:, 4:5], w["bg"]), (cols[:, 5:6], w["bo"]),
            (dmt[:, :, :], w["dmt"]), (dsum[:, :], w["dsum"]), (bdm[:, :], w["bdm"]), (hm[:, :], w["hm"]),
            (cols[:, 6:7], w["n0_g"]), (cols[:, 7:8], w["n0_b"]), (cols[:, 8:9], w["n1_g"]), (cols[:, 9:10], w["n1_b"]),
            (cols[:, 10:11], w["fc2_b"]), (wfc1[:, :], w["fc1"]), (wfc2[:, :, :], w["fc2"]), (bfc1[:, :], w["fc1_b"]),
            (lng[:, :], w["lng"]), (lnb[:, :], w["lnb"]), (jmat[:, :], w["jmat"]), (wrt[:, :], w["router"]),
            (brt[:, :], w["rbias"].to_broadcast([T, E])), (before[:, :], w["before"]), (all1[:, :], w["all1"]),
            (pick[:, :], w["pick"]),
        ]
        CONSTS = 16 * len(const_loads)
        SETUP_DVE = 8

        def pipeline(eng, body):
            body(-2, False, False, True)
            body(-1, False, True, True)
            body(0, True, True, True)
            with eng.Fori(1, GROUPS - 3, 2) as g:
                body(g, True, True, True, 1)
                body(g + 1, True, True, True, 0)
            body(GROUPS - 3, True, True, True)
            body(GROUPS - 2, True, True, False)
            body(GROUPS - 1, True, False, False)

        def pairs_before(g):
            return g * PAIRS

        def routed_before(g):
            return g * SHARED

        @block.sync
        def _(sp):
            sp.dma_start(xin[:, :], x[:, 0:GS, :].rearrange("p s t -> p (s t)")).then_inc(x_in, 16)
            for dst, src in const_loads:
                sp.dma_start(dst, src).then_inc(consts_in, 16)
            for n, (k, c, width) in enumerate(chunks):
                if n >= FC:
                    sp.wait_ge(setup_act, n - FC + 1)
                    sp.wait_ge(setup_pool, n - FC + 1)
                sp.dma_start(ff[:, n % FC, 0:width], w["experts"][:, k, c:c + width]).then_inc(stage_in[n % FC], 16)

            def load_x(a):
                sp.wait_ge(a_pe, did(A_PE, "zh", a - 1))
                sp.dma_start(xin[:, :], x[:, bass.ds(a * GS, GS), :].rearrange("p s t -> p (s t)")).then_inc(x_in, 16)

            def store(g):
                sp.wait_ge(out_ready, g + 1)
                par = sp_par[0]
                sp.dma_start(out[:, bass.ds(g * N, N)], h1[:, par, :]).then_inc(out_done, 16)

            sp_par = [0]

            def one(g, moe, stage_b, stage_a, par=None):
                if stage_a and from_group(g, -1):
                    load_x(g + 2)
                if moe and from_group(g, 1):
                    sp_par[0] = (1 - par) if par is not None else (g - 1) % 2
                    store(g - 1)
            pipeline(sp, one)
            sp_par[0] = (GROUPS - 1) % 2
            store(GROUPS - 1)
            sp.wait_ge(out_done, 16 * GROUPS)

        @block.tensor
        def _(pe):
            mm = nc.tensor.matmul

            def one_pass(outp, lhs, rhs, start=True, stop=True):
                return mm(outp, lhs, rhs, start=start, stop=stop)

            def center(dst, src):
                return mm(dst[:, 0:N], cmat[:, :], src, start=True, stop=True)

            def variance(dst, sq, n, start=True, stop=True):
                for s in range(GS):
                    last = mm(dst[0:T, s:s + 1], sq[:, s * T:(s + 1) * T], nth[:, n:n + 1], start=start and s == 0,
                              stop=stop and s == GS - 1, skip_group_check=True)
                return last

            def spread(dst, rs):
                for s in range(GS):
                    last = mm(dst[:, s * T:(s + 1) * T], rs[:, s:s + 1].to_broadcast([T, 128]), ident[:, :],
                              start=True, stop=True, is_transpose=True)
                return last

            def stage_a(p, a):
                if p == 0:
                    pe.wait_ge(x_in, 16 * (a + 1))
                    if from_group(a, 1):
                        pe.wait_ge(a_dve, did(A_DVE, "r", a - 1))
                    mm(zv[0], wtok[:, 0, :], xin[:, :], start=True, stop=True)
                    mm(zv[1], wtok[:, 1, :], xin[:, :], start=True, stop=True).then_inc(a_pe, 1)
                if p == 2:
                    pe.wait_ge(a_act, did(A_ACT, "zf", a))
                    mm(zv[0], wtok[:, 2, :], xin[:, :], start=True, stop=True).then_inc(a_pe, 1)
                if p == 17:
                    pe.wait_ge(a_dve, did(A_DVE, "h", a))
                    pe.wait_ge(a_act, did(A_ACT, "zh", a))
                    center(FA[0], h0[:, :]).then_inc(a_pe, 1)
                if p == 18:
                    pe.wait_ge(a_act, did(A_ACT, "sq", a))
                    variance(FA[1], tile[1], 0).then_inc(a_pe, 1)
                if p == 20:
                    pe.wait_ge(a_pool, did(A_POOL, "rs", a))
                    spread(FA[0], a_small[:, 1, 0:GS]).then_inc(a_pe, 1)
                if p == 21:
                    pe.wait_ge(a_dve, did(A_DVE, "src", a))
                    for s in range(GS):
                        last = mm(FA[s // 2][0:T, (s % 2) * 2 * D:(s % 2 + 1) * 2 * D], tile[2][:, s * T:(s + 1) * T],
                                  wkv[:, :], start=True, stop=True)
                    last.then_inc(a_pe, 1)
                if p == 22:
                    pe.wait_ge(a_dve, did(A_DVE, "kv", a))
                    mm(FA[0][:, 0:N], wqgo[:, 0, :], tile[2], start=True, stop=True)
                    mm(FA[1][:, 0:N], wqgo[:, 1, :], tile[2], start=True, stop=True).then_inc(a_pe, 1)
                if p == 23:
                    pe.wait_ge(a_act, did(A_ACT, "g", a))
                    for s in range(GS):
                        mm(FA[0][:, s * D:(s + 1) * D], kv[:, s, 0:D], kv[:, s, D:2 * D], start=True, stop=True)
                    for s in range(GS):
                        last = mm(FA[1][:, s:s + 1], kv[:, s, 0:D], ones[:, :], start=True, stop=True)
                    last.then_inc(a_pe, 1)
                if p == 24:
                    pe.wait_ge(a_dve, did(A_DVE, "bds", a))
                    for s in range(GS):
                        mm(FA[0][0:T, s * D:(s + 1) * D], tile[6][:, s * T:(s + 1) * T], bdv[:, s, :],
                           start=s == 0, stop=False, skip_group_check=True)
                    for h in range(HEADS):
                        mm(FA[0][0:T, :].rearrange("p (s c) -> p s c", c=D)[:, :, h * KD:(h + 1) * KD], dmt[:, h, :],
                           kv[:, :, D + h * KD:D + (h + 1) * KD], start=False, stop=h == HEADS - 1, skip_group_check=True)
                    for s in range(GS):
                        last = mm(FA[1][0:T, s * HEADS:(s + 1) * HEADS], tile[6][:, s * T:(s + 1) * T],
                                  bds[:, s * HEADS:(s + 1) * HEADS], start=True, stop=True)
                    last.then_inc(a_pe, 1)
                if p == 30:
                    pe.wait_ge(a_dve, did(A_DVE, "on", a))
                    for s in range(GS):
                        last = nc.tensor.transpose(FA[0][:, s * T:(s + 1) * T], oc[:, s * D:(s + 1) * D], ident[:, :])
                    last.then_inc(a_pe, 1)
                if p == 31:
                    pe.wait_ge(a_dve, did(A_DVE, "og", a))
                    mm(FA[1][:, 0:N], wqgo[:, 2, :], tile[1], start=True, stop=True).then_inc(a_pe, 1)

            def stage_b(p, b, par):
                if p == 0:
                    pe.wait_ge(a_dve, did(A_DVE, "r", b))
                    if from_group(b, 1):
                        pe.wait_ge(b_dve, did(B_DVE, "gt_lo", b - 1))
                    center(FB, r_t[:, :]).then_inc(b_pe, 1)
                if p == 1:
                    pe.wait_ge(b_act, did(B_ACT, "sq0", b))
                    variance(FB, b_sq[:, 0, :], 0).then_inc(b_pe, 1)
                if p == 3:
                    pe.wait_ge(b_pool, did(B_POOL, "rs0", b))
                    spread(FB, b_small[:, 1, 0:GS]).then_inc(b_pe, 1)
                for j in range(FC):
                    if p == 4 + j:
                        pe.wait_ge(b_dve, did(B_DVE, "x1", b))
                        if j:
                            pe.wait_ge(b_act, did(B_ACT, f"hp{j - 1}", b))
                        mm(FB[:, 0:N], wfc1[:, j * D:(j + 1) * D], b_x1[:, :], start=True, stop=True).then_inc(b_pe, 1)
                if p == 11:
                    pe.wait_ge(b_dve, did(B_DVE, "hs2", b))
                    mm(FB[:, 0:N], jmat[:, :], b_mix[:, :], start=True, stop=True).then_inc(b_pe, 1)
                if p == 13:
                    pe.wait_ge(b_act, did(B_ACT, "fsq1", b))
                    pe.wait_ge(b_dve, did(B_DVE, "c_3", b))
                    variance(FB, b_sq[:, 0, :], 1, start=True, stop=False)
                    variance(FB, b_sq[:, 1, :], 1, start=False, stop=False).then_inc(b_pe, 1)
                if p == 14:
                    pe.wait_ge(b_act, did(B_ACT, "fsq3", b))
                    variance(FB, b_sq[:, 0, :], 1, start=False, stop=False)
                    variance(FB, b_sq[:, 1, :], 1, start=False, stop=True).then_inc(b_pe, 1)
                if p == 16:
                    pe.wait_ge(b_pool, did(B_POOL, "rs1", b))
                    spread(FB, b_small[:, 3, 0:GS]).then_inc(b_pe, 1)
                if p == 17:
                    pe.wait_ge(b_act, did(B_ACT, "rsb", b))
                    for j in range(FC):
                        last = mm(FB[:, 0:N], wfc2[:, j, :], ff_tile[j], start=j == 0, stop=j == FC - 1)
                    last.then_inc(b_pe, 1)
                if p == 18:
                    pe.wait_ge(b_dve, did(B_DVE, "r2", b))
                    center(FB, b_mix[:, :]).then_inc(b_pe, 1)
                if p == 19:
                    pe.wait_ge(b_act, did(B_ACT, "sq2", b))
                    variance(FB, b_sq[:, 0, :], 0).then_inc(b_pe, 1)
                if p == 21:
                    pe.wait_ge(b_pool, did(B_POOL, "rs2", b))
                    spread(FB, b_small[:, 5, 0:GS]).then_inc(b_pe, 1)
                if p == 22:
                    pe.wait_ge(b_dve, did(B_DVE, "h1", b))
                    center(FB, h1[:, par, :]).then_inc(b_pe, 1)
                if p == 23:
                    pe.wait_ge(b_act, did(B_ACT, "sq3", b))
                    variance(FB, b_sq[:, 0, :], 0).then_inc(b_pe, 1)
                if p == 25:
                    pe.wait_ge(b_pool, did(B_POOL, "rs3", b))
                    spread(FB, b_small[:, 7, 0:GS]).then_inc(b_pe, 1)
                if p == 27:
                    pe.wait_ge(b_dve, did(B_DVE, "xf", b))
                    for s in range(GS):
                        last = mm(FB[0:T, s * E:(s + 1) * E], b_c[:, s * T:(s + 1) * T], wrt[:, :], start=True, stop=True)
                    last.then_inc(b_pe, 1)
                if p == 28:
                    pe.wait_ge(b_dve, did(B_DVE, "mask", b))
                    first = True
                    for s in range(GS + 1):
                        for earlier in range(s):
                            last = mm(FB[0:T, s * E:(s + 1) * E], all1[:, :], mask[:, earlier, :], start=first, stop=False,
                                      skip_group_check=True)
                            first = False
                        if s < GS:
                            last = mm(FB[0:T, s * E:(s + 1) * E], before[:, :], mask[:, s, :], start=first, stop=False,
                                      skip_group_check=True)
                            first = False
                    last.then_inc(b_pe, 1)
                if p == 31:
                    pe.wait_ge(b_dve, did(B_DVE, "gate", b))
                    for s in range(GS):
                        last = nc.tensor.transpose(FB[:, s * T:(s + 1) * T], g2[:, s, :], ident[:, :])
                    last.then_inc(b_pe, 1)

            def product(dst, kind, p, hi, lo, start, stop):
                cs = slice(p * 128, (p + 1) * 128)
                mm(dst[:, 0:N], whi[:, kind, cs], hi, start=start, stop=False)
                mm(dst[:, 0:N], wlo[:, kind, cs], hi, start=False, stop=False)
                return mm(dst[:, 0:N], whi[:, kind, cs], lo, start=False, stop=stop)

            def down(p, g, n, buf):
                pe.wait_ge(hl_done, n + 1)
                if p == 0 and from_group(g, 1):
                    pe.wait_ge(out_ready, g)
                product(ACC, 2, p, hh[:, buf, :], hl[:, buf, :], p == 0, p == SHARED).then_inc(down_done, 1)

            def one(g, moe, with_b, with_a, par=None):
                if par is None:
                    par = g % 2
                for p in range(PAIRS):
                    if moe:
                        n = pairs_before(g) + p
                        b2 = (par + p) % 2
                        if p == 0:
                            pe.wait_ge(b_pool, did(B_POOL, "xl", g))
                        if from_group(g, 1) or p >= 2:
                            pe.wait_ge(silu_done, n - 1)
                        product(PG[b2], 0, p, xh[:, par, :], xl[:, par, :], True, True).then_inc(gate_done, 1)
                        if p >= 1:
                            pe.wait_ge(prod_done, routed_before(g) + p)
                        elif from_group(g, 1):
                            pe.wait_ge(h_done, n)
                        product(PU, 1, p, xh[:, par, :], xl[:, par, :], True, True).then_inc(up_done, 1)
                        if p != SHARED:
                            if p == 0:
                                pe.wait_ge(b_dve, did(B_DVE, "gt_lo", g))
                            if from_group(g, 1) or p >= 1:
                                pe.wait_ge(h_done, n)
                            mm(PB[:, 0:N], pick[:, p * 128:(p + 1) * 128], gt[:, :], start=True, stop=True)\
                                .then_inc(spread_done, 1)
                        if p >= LAG:
                            down(p - LAG, g, n - LAG, b2)
                        elif from_group(g, 1):
                            down(PAIRS + p - LAG, g - 1, n - LAG, b2)
                    if with_b:
                        stage_b(p, g + 1, 1 - par)
                    if with_a:
                        stage_a(p, g + 2)

            pe.wait_ge(consts_in, CONSTS)
            pe.wait_ge(setup_dve, SETUP_DVE - 1)
            for j in range(FC):
                last = mm(FB[:, 0:1], wfc2[:, j, :], lnb[:, j:j + 1], start=j == 0, stop=j == FC - 1)
            last.then_inc(setup_pe, 1)
            pe.wait_ge(setup_dve, SETUP_DVE + 1)
            pe.wait_ge(setup_pool, len(chunks))
            pe.wait_ge(setup_act, len(chunks))
            pipeline(pe, one)
            for p in range(PAIRS - LAG, PAIRS):
                n = (GROUPS - 1) * PAIRS + p
                down(p, GROUPS - 1, n, n % 2)

        @block.scalar
        def _(act):
            go = nc.scalar.activation

            def stage_a(p, a):
                if p == 1:
                    act.wait_ge(a_pe, did(A_PE, "zf_zi", a))
                    go(body(tile[0]), zs[0], ACT.Identity, bias=col["bf"]).then_inc(a_act, 1)
                    go(body(tile[1]), zs[1], ACT.Identity, bias=col["bi"]).then_inc(a_act, 1)
                if p == 3:
                    act.wait_ge(a_pe, did(A_PE, "zh", a))
                    go(body(tile[2]), zs[0], ACT.Identity, bias=col["bh"]).then_inc(a_act, 1)
                    act.wait_ge(a_dve, did(A_DVE, "mi", a))
                    go(body(tile[0]), body(tile[0]), ACT.Abs)
                    go(body(tile[1]), body(tile[1]), ACT.Abs).then_inc(a_act, 1)
                if p == 7:
                    act.wait_ge(a_act, did(A_ACT, "abs", a))
                    act.wait_ge(a_dve, did(A_DVE, "em", a))
                    for t, sign in ((tile[0], -1.0), (tile[1], -1.0), (tile[5], 1.0), (tile[4], 1.0), (step_t[:, :], 1.0),
                                    (tile[7], 1.0), (tile[3], -1.0), (tile[2], 1.0)):
                        last = go(body(t), body(t), ACT.Exp, scale=sign)
                    last.then_inc(a_act, 1)
                if p == 18:
                    act.wait_ge(a_pe, did(A_PE, "center", a))
                    go(tile[0], FA[0][:, 0:N], ACT.Copy).then_inc(a_act, 1)
                    go(tile[1], FA[0][:, 0:N], ACT.Square).then_inc(a_act, 1)
                if p == 23:
                    act.wait_ge(a_pe, did(A_PE, "qg", a))
                    go(tile[6], FA[0][:, 0:N], ACT.Identity, bias=col["bq"]).then_inc(a_act, 1)
                    go(tile[7], FA[1][:, 0:N], ACT.Silu, bias=col["bg"]).then_inc(a_act, 1)
                if p == 26:
                    act.wait_ge(a_dve, did(A_DVE, "oc", a))
                    go(osq, oc, ACT.Square).then_inc(a_act, 1)

            def center_square(pe_step, b):
                act.wait_ge(b_pe, did(B_PE, pe_step, b))
                go(b_c[:, :], FB[:, 0:N], ACT.Copy).then_inc(b_act, 1)
                go(b_sq[:, 0, :], FB[:, 0:N], ACT.Square).then_inc(b_act, 1)

            def stage_b(p, b, par):
                if p == 1:
                    center_square("center0", b)
                    if from_group(b, 1):
                        act.wait_ge(b_dve, did(B_DVE, "h1", b - 1))
                    go(hb[:, :], h0[:, :], ACT.Identity, bias=col["n1_b"]).then_inc(b_act, 1)
                for j in range(FC):
                    if p == 5 + j:
                        act.wait_ge(b_pe, did(B_PE, f"fc1_{j}", b))
                        go(ff_tile[j], FB[:, 0:N], ACT.Identity, bias=bfc1[:, j:j + 1]).then_inc(b_act, 1)
                if p == 9:
                    act.wait_ge(b_act, did(B_ACT, "hp3", b))
                    for j in range(FC):
                        last = go(ff_tile[j], ff_tile[j], ACT.Gelu)
                    last.then_inc(b_act, 1)
                if p == 12:
                    for j in (0, 1):
                        act.wait_ge(b_dve, did(B_DVE, f"c_{j}", b))
                        go(b_sq[:, j, :], ff_tile[j], ACT.Square).then_inc(b_act, 1)
                if p == 13:
                    act.wait_ge(b_pe, did(B_PE, "var1a", b))
                    for j in (2, 3):
                        act.wait_ge(b_dve, did(B_DVE, f"c_{j}", b))
                        go(b_sq[:, j - 2, :], ff_tile[j], ACT.Square).then_inc(b_act, 1)
                if p == 17:
                    act.wait_ge(b_pe, did(B_PE, "spread1", b))
                    go(b_mix[:, :], FB[:, 0:N], ACT.Copy).then_inc(b_act, 1)
                if p == 19:
                    center_square("center2", b)
                if p == 23:
                    center_square("center3", b)
                if p == 26:
                    act.wait_ge(b_dve, did(B_DVE, "xf", b))
                    if from_group(b, 2):
                        act.wait_ge(up_done, pairs_before(b - 1))
                    go(xh[:, par, :], b_c[:, :], ACT.Copy).then_inc(b_act, 1)
                if p == 29:
                    act.wait_ge(b_dve, did(B_DVE, "shift", b))
                    go(ee, ee, ACT.Exp).then_inc(b_act, 1)

            def split_h(n, buf, has_down):
                act.wait_ge(h_done, n + 1)
                if has_down:
                    act.wait_ge(down_done, n - 1)
                go(hh[:, buf, :], h_t[:, buf, :], ACT.Copy).then_inc(hh_done, 1)

            def one(g, moe, with_b, with_a, par=None):
                if par is None:
                    par = g % 2
                for p in range(PAIRS):
                    if moe:
                        n = pairs_before(g) + p
                        b2 = (par + p) % 2
                        act.wait_ge(gate_done, n + 1)
                        if p == 1 and from_group(g, 1):
                            act.wait_ge(h_done, n - 1)
                        elif p != 1 and (from_group(g, 1) or p >= 2):
                            act.wait_ge(prod_done, routed_before(g) + p - 1)
                        go(s_t[:, b2, :], PG[b2][:, 0:N], ACT.Silu).then_inc(silu_done, 1)
                        if from_group(g, 1) or p >= 1:
                            split_h(n - 1, 1 - b2, from_group(g, 1) or p >= 3)
                    if with_b:
                        stage_b(p, g + 1, 1 - par)
                    if with_a:
                        stage_a(p, g + 2)

            for n, (k, c, width) in enumerate(chunks):
                act.wait_ge(stage_in[n % FC], 16 * (n // FC + 1))
                go(whi[:, k, c:c + width], ff[:, n % FC, 0:width], ACT.Copy).then_inc(setup_act, 1)
            act.wait_ge(consts_in, CONSTS)
            act.wait_ge(setup_dve, 7)
            pipeline(act, one)
            n = GROUPS * PAIRS - 1
            split_h(n, n % 2, True)

        @block.gpsimd
        def _(pool):
            def power(sem_done, dst, src, width):
                pool.tensor_tensor(dst, src, mhalf[:, 0:width], ALU.pow).then_inc(sem_done, 1)

            def stage_a(p, a):
                if p == 19:
                    pool.wait_ge(a_dve, did(A_DVE, "ve", a))
                    power(a_pool, a_small[:, 1, 0:GS], a_small[:, 0, 0:GS], GS)
                if p == 27:
                    pool.wait_ge(a_dve, did(A_DVE, "ove", a))
                    power(a_pool, a_small[:, 5, :], a_small[:, 4, :], GS * HEADS)

            def stage_b(p, b, par):
                for i, at in enumerate((2, 15, 20, 24)):
                    if p == at:
                        pool.wait_ge(b_dve, did(B_DVE, f"ve{i}", b))
                        power(b_pool, b_small[:, 2 * i + 1, 0:GS], b_small[:, 2 * i, 0:GS], GS)
                if p == 26:
                    pool.wait_ge(b_act, did(B_ACT, "xh", b))
                    pool.tensor_tensor(xl[:, par, :], b_c[:, :], xh[:, par, :].bitcast(fp32), ALU.subtract)\
                        .then_inc(b_pool, 1)

            def one(g, moe, with_b, with_a, par=None):
                if par is None:
                    par = g % 2
                for p in range(PAIRS):
                    if moe:
                        n = pairs_before(g) + p
                        b2 = (par + p) % 2
                        pool.wait_ge(hh_done, n + 1)
                        if from_group(g, 1) or p >= 2:
                            pool.wait_ge(down_done, n - 1)
                        pool.tensor_tensor(hl[:, b2, :], h_t[:, b2, :], hh[:, b2, :].bitcast(fp32), ALU.subtract)\
                            .then_inc(hl_done, 1)
                    if with_b:
                        stage_b(p, g + 1, 1 - par)
                    if with_a:
                        stage_a(p, g + 2)

            for n, (k, c, width) in enumerate(chunks):
                pool.wait_ge(setup_act, n + 1)
                pool.tensor_tensor(wlo[:, k, c:c + width], ff[:, n % FC, 0:width],
                                   whi[:, k, c:c + width].bitcast(fp32), ALU.subtract).then_inc(setup_pool, 1)
            pool.wait_ge(setup_dve, 7)
            pipeline(pool, one)

        @block.vector
        def _(dve):
            tt, ts, stt = dve.tensor_tensor, dve.tensor_scalar, dve.scalar_tensor_tensor
            add, sub, mul = ALU.add, ALU.subtract, ALU.mult

            def stage_a(p, a):
                def after(step):
                    dve.wait_ge(a_dve, did(A_DVE, step, a))
                B = [body(t) for t in tile]
                if p == 2:
                    dve.wait_ge(a_act, did(A_ACT, "zf", a))
                    ts(B[3], B[0], 0.0, None, ALU.min).then_inc(a_dve, 1)
                    dve.wait_ge(a_act, did(A_ACT, "zi", a))
                    ts(B[4], B[1], 0.0, None, ALU.min).then_inc(a_dve, 1)
                if p == 3:
                    dve.wait_ge(a_act, did(A_ACT, "zh", a))
                    ts(B[5], B[2], 0.0, None, ALU.min).then_inc(a_dve, 1)
                    ts(B[6], B[2], 0.0, 2.0, ALU.max, mul).then_inc(a_dve, 1)
                if p == 4:
                    after("mi")
                    tt(B[3], B[4], B[3], sub).then_inc(a_dve, 1)
                    after("d")
                    tt(body(e_t[:, :]), B[3], B[5], add).then_inc(a_dve, 1)
                if p == 5:
                    after("e")
                    dve.tensor_tensor_scan(tile[4], keepm[:, :], e_t[:, :], 0.0, mul, ALU.max).then_inc(a_dve, 1)
                    after("n2")
                    ts(B[2], B[3], 0.0, None, ALU.min).then_inc(a_dve, 1)
                    after("nd")
                    ts(B[3], B[3], 0.0, None, ALU.max).then_inc(a_dve, 1)
                if p == 6:
                    after("rd")
                    tt(B[7], B[4], B[3], sub).then_inc(a_dve, 1)
                    tt(body(step_t[:, :]), seqs(tile[4])[:, :, 0:T_IN], B[4], sub).then_inc(a_dve, 1)
                    after("dm")
                    tt(B[4], body(e_t[:, :]), B[4], sub).then_inc(a_dve, 1)
                if p == 8:
                    dve.wait_ge(a_act, did(A_ACT, "exps", a))
                    ts(B[1], B[1], 1.0, None, add).then_inc(a_dve, 1)
                    ts(B[0], B[0], 1.0, None, add).then_inc(a_dve, 1)
                    after("ti")
                    stt(B[5], B[5], 1.0, B[1], add, mul).then_inc(a_dve, 1)
                if p == 9:
                    after("tf")
                    stt(B[6], B[6], 1.0, B[0], add, mul).then_inc(a_dve, 1)
                    tt(B[3], B[3], B[1], mul).then_inc(a_dve, 1)
                if p == 10:
                    tt(B[2], B[2], B[0], mul).then_inc(a_dve, 1)
                    after("b")
                    tt(B[3], B[3], B[2], add).then_inc(a_dve, 1)
                    after("den")
                    tt(B[2], B[3], B[5], mul).then_inc(a_dve, 1)
                if p in (11, 12):
                    after("pd")
                    half = B[2][:, (p - 11) * 2:(p - 11) * 2 + 2, :]
                    dve.reciprocal(half, half).then_inc(a_dve, 1)
                if p == 13:
                    after("r2")
                    tt(B[6], B[6], B[2], mul).then_inc(a_dve, 1)
                    after("mv1")
                    tt(B[6], B[6], B[3], mul).then_inc(a_dve, 1)
                if p == 14:
                    after("mv2")
                    tt(body(val_t[:, :]), B[6], B[4], mul).then_inc(a_dve, 1)
                    after("val")
                    dve.tensor_tensor_scan(tile[0], step_t[:, :], val_t[:, :], 0.0, mul, add).then_inc(a_dve, 1)
                if p == 15:
                    after("s")
                    tt(B[7], B[7], B[0], mul).then_inc(a_dve, 1)
                    after("h1")
                    tt(B[7], B[7], B[1], mul).then_inc(a_dve, 1)
                if p == 16:
                    after("h2")
                    tt(B[7], B[7], B[2], mul).then_inc(a_dve, 1)
                    after("h3")
                    if from_group(a, 1):
                        dve.wait_ge(b_act, did(B_ACT, "hb", a - 1))
                    tt(body(h0[:, :]), B[7], B[5], mul).then_inc(a_dve, 1)
                if p == 18:
                    dve.wait_ge(a_pe, did(A_PE, "var", a))
                    ts(a_small[:, 0, 0:GS], FA[1][0:T, 0:GS], 1e-5, None, add).then_inc(a_dve, 1)
                if p == 20:
                    dve.wait_ge(a_pe, did(A_PE, "spread", a))
                    tt(tile[2], tile[0], FA[0][:, 0:N], mul).then_inc(a_dve, 1)
                if p == 21:
                    dve.wait_ge(a_pe, did(A_PE, "kv", a))
                    bias2 = bkv[:, :].unsqueeze(1).to_broadcast([T, 2, 2 * D])
                    for i in (0, 1):
                        last = tt(kv[:, 2 * i:2 * i + 2, :], FA[i][0:T, :].rearrange("p (s c) -> p s c", c=2 * D), bias2, add)
                    last.then_inc(a_dve, 1)
                if p == 23:
                    dve.wait_ge(a_pe, did(A_PE, "outer", a))
                    tt(bdv, FA[0][:, :].rearrange("p (s c) -> p s c", c=D),
                       bdm[:, :].unsqueeze(1).to_broadcast([D, GS, D]), mul).then_inc(a_dve, 1)
                    tt(bds[:, :].rearrange("p (s h) -> p s h", h=HEADS), FA[1][:, 0:GS].unsqueeze(2).to_broadcast([D, GS, HEADS]),
                       hm[:, :].unsqueeze(1).to_broadcast([D, GS, HEADS]), mul).then_inc(a_dve, 1)
                if p == 24:
                    dve.wait_ge(a_pe, did(A_PE, "mix", a))
                    dve.tensor_reduce(a_small[:, 2, :], heads(FA[0][0:T, :]), AX, add).then_inc(a_dve, 1)
                    after("mu")
                    stt(heads(oc), over_heads(a_small[:, 2, :]), -1.0 / KD, heads(FA[0][0:T, :]), mul, add).then_inc(a_dve, 1)
                if p == 25:
                    tt(a_small[:, 3, :].rearrange("p (s h) -> p s h", h=HEADS),
                       FA[1][0:T, 0:GS * HEADS].rearrange("p (s h) -> p s h", h=HEADS),
                       dsum[:, :].unsqueeze(1).to_broadcast([T, GS, HEADS]), add).then_inc(a_dve, 1)
                    after("den1")
                    stt(a_small[:, 3, :], a_small[:, 3, :], -1.0, a_small[:, 3, :], mul, ALU.max).then_inc(a_dve, 1)
                    after("den2")
                    ts(a_small[:, 3, :], a_small[:, 3, :], 1.0, None, ALU.max).then_inc(a_dve, 1)
                    after("den3")
                    stt(a_small[:, 3, :], a_small[:, 3, :], 1e-6, a_small[:, 3, :], mul, mul).then_inc(a_dve, 1)
                if p == 26:
                    dve.wait_ge(a_act, did(A_ACT, "osq", a))
                    dve.tensor_reduce(a_small[:, 2, :], heads(osq), AX, add).then_inc(a_dve, 1)
                    after("ovar")
                    stt(a_small[:, 4, :], a_small[:, 2, :], 1.0 / KD, a_small[:, 3, :], mul, add).then_inc(a_dve, 1)
                if p == 30:
                    dve.wait_ge(a_pool, did(A_POOL, "ors", a))
                    tt(heads(oc), heads(oc), over_heads(a_small[:, 5, :]), mul).then_inc(a_dve, 1)
                    dve.wait_ge(a_pe, did(A_PE, "turn", a))
                    tt(tile[1], tile[7], FA[0][:, 0:N], mul).then_inc(a_dve, 1)
                if p == 32:
                    dve.wait_ge(a_pe, did(A_PE, "wo", a))
                    if from_group(a, 1):
                        dve.wait_ge(b_pe, did(B_PE, "center0", a - 1))
                    stt(r_t[:, :], FA[1][:, 0:N], col["bo"], tile[2], add, add).then_inc(a_dve, 1)

            def stage_b(p, b, par):
                def after(step):
                    dve.wait_ge(b_dve, did(B_DVE, step, b))

                def var_eps(i, pe_step, eps):
                    dve.wait_ge(b_pe, did(B_PE, pe_step, b))
                    ts(b_small[:, 2 * i, 0:GS], FB[0:T, 0:GS], eps, None, add).then_inc(b_dve, 1)
                if p == 1:
                    var_eps(0, "var0", 1e-5)
                if p == 3:
                    dve.wait_ge(b_pe, did(B_PE, "spread0", b))
                    tt(b_x1[:, :], b_c[:, :], FB[:, 0:N], mul).then_inc(b_dve, 1)
                    after("t0")
                    ts(b_x1[:, :], b_x1[:, :], col["n0_g"], col["n0_b"], mul, add).then_inc(b_dve, 1)
                if p == 10:
                    dve.wait_ge(b_act, did(B_ACT, "gelu", b))
                    tt(b_mix[:, :], ff_tile[0], ff_tile[1], add).then_inc(b_dve, 1)
                    after("hs0")
                    tt(b_mix[:, :], b_mix[:, :], ff_tile[2], add).then_inc(b_dve, 1)
                    after("hs1")
                    tt(b_mix[:, :], b_mix[:, :], ff_tile[3], add).then_inc(b_dve, 1)
                if p in (11, 12):
                    dve.wait_ge(b_pe, did(B_PE, "mean", b))
                    for j in (2 * (p - 11), 2 * (p - 11) + 1):
                        tt(ff_tile[j], ff_tile[j], FB[:, 0:N], sub).then_inc(b_dve, 1)
                if p == 14:
                    var_eps(1, "var1b", 1e-6)
                if p == 17:
                    dve.wait_ge(b_pe, did(B_PE, "fc2", b))
                    tt(b_mix[:, :], b_mix[:, :], FB[:, 0:N], mul).then_inc(b_dve, 1)
                    after("r2a")
                    stt(b_mix[:, :], b_mix[:, :], cb[:, :], b_x1[:, :], add, add).then_inc(b_dve, 1)
                if p == 19:
                    var_eps(2, "var2", 1e-5)
                if p == 21:
                    dve.wait_ge(b_pe, did(B_PE, "spread2", b))
                    tt(b_x1[:, :], b_c[:, :], FB[:, 0:N], mul).then_inc(b_dve, 1)
                    after("y")
                    if from_group(b, 2):
                        dve.wait_ge(out_done, 16 * (b - 1))
                    stt(h1[:, par, :], b_x1[:, :], col["n1_g"], hb[:, :], mul, add).then_inc(b_dve, 1)
                if p == 23:
                    var_eps(3, "var3", 1e-5)
                if p == 25:
                    dve.wait_ge(b_pe, did(B_PE, "spread3", b))
                    tt(b_c[:, :], b_c[:, :], FB[:, 0:N], mul).then_inc(b_dve, 1)
                if p == 27:
                    dve.wait_ge(b_pe, did(B_PE, "router", b))
                    tt(lg[:, :, 0:E], router_out, brt[:, :].unsqueeze(1).to_broadcast([T, GS, E]), add).then_inc(b_dve, 1)
                    after("lg")
                    dve.memset(carrier[:, 0:1], 0.0)
                    for s in range(GS):
                        last = dve.max(top[:, s, :], lg[:, s, 0:E])
                    last.then_inc(b_dve, 1)
                    after("top")
                    dve.memset(top[:, :, TOP_K:8], BIG).then_inc(b_dve, 1)
                if p == 28:
                    after("big")
                    dve.memset(carrier[:, 1:2], 0.0)
                    for s in range(GS):
                        last = dve.match_replace(matched[:, s, :], top[:, s, :], lg[:, s, :], -BIG)
                    last.then_inc(b_dve, 1)
                    after("match")
                    tt(mask[:, :, :], matched[:, :, 0:E], lg[:, :, 0:E], ALU.not_equal).then_inc(b_dve, 1)
                    tt(ee, lg[:, :, 0:E], per_seq(top[:, :, 0]), sub).then_inc(b_dve, 1)
                if p == 29:
                    dve.wait_ge(b_act, did(B_ACT, "exp", b))
                    dve.tensor_reduce(b_small[:, 0, 4:8], ee, AX, add).then_inc(b_dve, 1)
                    tt(gk, ee, mask[:, :, :], mul).then_inc(b_dve, 1)
                    after("em")
                    dve.tensor_reduce(b_small[:, 1, 4:8], gk, AX, add).then_inc(b_dve, 1)
                if p == 30:
                    dve.wait_ge(b_pe, did(B_PE, "rank", b))
                    stt(ee, router_out, float(CAPACITY), nrun[:, :].unsqueeze(1).to_broadcast([T, GS, E]), sub, ALU.is_lt)\
                        .then_inc(b_dve, 1)
                    after("keep")
                    tt(nrun[:, :], nrun[:, :], FB[0:T, GS * E:(GS + 1) * E], sub).then_inc(b_dve, 1)
                    after("sum")
                    stt(b_small[:, 2, 4:8], b_small[:, 0, 4:8], 1e-9, b_small[:, 1, 4:8], mul, add).then_inc(b_dve, 1)
                    after("tot")
                    dve.reciprocal(b_small[:, 3, 4:8], b_small[:, 2, 4:8]).then_inc(b_dve, 1)
                    tt(gk, gk, ee, mul).then_inc(b_dve, 1)
                    after("gk")
                    for half in (0, 1):
                        last = tt(g2[:, :, half * E:(half + 1) * E], gk, per_seq(b_small[:, 3, 4:8]), mul)
                    last.then_inc(b_dve, 1)
                if p == 32:
                    dve.wait_ge(b_pe, did(B_PE, "turn", b))
                    if from_group(b, 1):
                        dve.wait_ge(spread_done, b * SHARED)
                    dve.tensor_copy(gt[:, :], FB[:, 0:N]).then_inc(b_dve, 1)
                    after("gt_hi")
                    tt(gt[E:2 * E, :], FB[E:2 * E, 0:N], gt[E:2 * E, :], sub).then_inc(b_dve, 1)

            def finish(g, par):
                dve.wait_ge(down_done, pairs_before(g + 1))
                tt(h1[:, par, :], h1[:, par, :], ACC[:, 0:N], add).then_inc(out_ready, 1)

            def one(g, moe, with_b, with_a, par=None):
                if par is None:
                    par = g % 2
                for p in range(PAIRS):
                    if moe:
                        n = pairs_before(g) + p
                        b2 = (par + p) % 2
                        dve.wait_ge(silu_done, n + 1)
                        dve.wait_ge(up_done, n + 1)
                        if p != SHARED:
                            if from_group(g, 1) or p >= 1:
                                dve.wait_ge(h_done, n)
                            tt(t_t[:, :], s_t[:, b2, :], PU[:, 0:N], mul).then_inc(prod_done, 1)
                            dve.wait_ge(prod_done, routed_before(g) + p + 1)
                            dve.wait_ge(spread_done, routed_before(g) + p + 1)
                            if from_group(g, 1) or p >= 2:
                                dve.wait_ge(hl_done, n - 1)
                            tt(h_t[:, b2, :], t_t[:, :], PB[:, 0:N], mul).then_inc(h_done, 1)
                        else:
                            dve.wait_ge(hl_done, n - 1)
                            stt(h_t[:, b2, :], s_t[:, b2, :], 0.5, PU[:, 0:N], mul, mul).then_inc(h_done, 1)
                        if p == LAG - 1 and from_group(g, 1):
                            finish(g - 1, 1 - par)
                    if with_b:
                        stage_b(p, g + 1, 1 - par)
                    if with_a:
                        stage_a(p, g + 2)

            dve.memset(e_t[:, :], 0.0)
            dve.memset(step_t[:, :], 0.0)
            dve.memset(val_t[:, :], 0.5)
            dve.memset(h0[:, :], 0.5).then_inc(setup_dve, 4)
            dve.memset(ones[:, :], 1.0)
            dve.memset(mhalf[:, :], -0.5)
            dve.memset(nrun[:, :], 0.0)
            dve.memset(lg[:, :, E:E + 2], BIG).then_inc(setup_dve, 3)
            dve.wait_ge(setup_dve, 7)
            dve.wait_ge(consts_in, CONSTS)
            dve.wait_ge(setup_pe, 1)
            for j in range(FC):
                last = ts(wfc2[:, j, :], wfc2[:, j, :], lng[:, j:j + 1], None, mul)
            last.then_inc(setup_dve, 1)
            tt(cb[:, :], FB[:, 0:1], col["fc2_b"], add).then_inc(setup_dve, 1)
            dve.wait_ge(setup_dve, SETUP_DVE + 1)
            pipeline(dve, one)
            finish(GROUPS - 1, (GROUPS - 1) % 2)


def kernel(**inputs):
    import numpy as np
    import concourse.bacc as bacc
    from concourse import mybir as mb
    from concourse.bass_utils import run_bass_kernel_spmd as run

    def c(a):
        return np.ascontiguousarray(a)

    i = {k: np.asarray(v) for k, v in inputs.items()}
    column = lambda a: c(a.reshape(-1, 1))
    f32 = np.float32
    experts = np.empty((128, 3, PAIRS * 128), f32)
    for kind, (routed, shared) in enumerate((("w_gate", "shared_w_gate"), ("w_up", "shared_w_up"))):
        experts[:, kind, :E * F] = i["L0_ffn_" + routed].reshape(E * F, D).T
        experts[:, kind, E * F:] = i["L0_ffn_" + shared].reshape(2 * F, D).T
    for lo, a in ((0, i["L0_ffn_w_down"]), (SHARED, i["L0_ffn_shared_w_down"])):
        n = a.shape[0] // 2
        experts[:, 2, lo * 128:(lo + n) * 128] = a.reshape(n, 2, D, F).transpose(1, 3, 0, 2).reshape(128, n * D)

    step = np.arange(T)
    diff = (step[:, None] - step[None, :]).astype(f32)
    decay = np.log(f32(1) - f32(2) ** (f32(-5) - np.arange(HEADS, dtype=f32))).astype(f32)
    dm = np.where(diff[None] >= 0, np.exp(diff[None] * decay[:, None, None]), 0).astype(f32)
    dm = dm / np.sqrt(dm.sum(-1, keepdims=True))
    head = np.arange(D) // KD
    keepm = np.ones((D, GS, T), f32)
    keepm[:, :, 0] = 0
    scale = KD ** -0.5
    import ml_dtypes
    arrays = {
        "x": c(i["x"].transpose(2, 0, 1)),
        "experts": experts,
        "wf": c(i["L0_tok_Wf"]), "wi": c(i["L0_tok_Wi"]), "wh": c(i["L0_tok_Wh"]),
        "bf": column(i["L0_tok_bf"]), "bi": column(i["L0_tok_bi"]), "bh": column(i["L0_tok_bh"]),
        "wq": c(i["L0_attn_wq"].T), "wg": c(i["L0_attn_wg"].T), "wo": c(i["L0_attn_wo"].T),
        "wk": c(i["L0_attn_wk"].T), "wv": c(i["L0_attn_wv"].T),
        "bq": column(i["L0_attn_bq"]), "bg": column(i["L0_attn_bg"]), "bo": column(i["L0_attn_bo"]),
        "bk": i["L0_attn_bk"].reshape(1, D), "bv": i["L0_attn_bv"].reshape(1, D),
        "n0_g": column(i["L0_attn_n0_g"]), "n0_b": column(i["L0_attn_n0_b"]),
        "n1_g": column(i["L0_attn_n1_g"]), "n1_b": column(i["L0_attn_n1_b"]),
        "fc1": c(i["L0_attn_fc1_w"].T), "fc1_b": c(i["L0_attn_fc1_b"].reshape(FC, D).T),
        "fc2": c(i["L0_attn_fc2_w"].reshape(D, FC, D).transpose(2, 1, 0)), "fc2_b": column(i["L0_attn_fc2_b"]),
        "lng": c(i["L0_attn_ln_ffn_g"].reshape(FC, D).T), "lnb": c(i["L0_attn_ln_ffn_b"].reshape(FC, D).T),
        "router": c(i["L0_ffn_router_w"].T), "rbias": i["L0_ffn_bias"].reshape(1, E),
        "cmat": (np.eye(D) - 1.0 / D).astype(f32), "jmat": np.full((D, D), 1.0 / (FC * D), f32),
        "nth": np.tile(np.array([[1.0 / D, 1.0 / (FC * D)]], f32), (D, 1)), "ident": np.eye(T, dtype=f32),
        "dmt": c(dm.transpose(2, 0, 1)), "dsum": c(dm.sum(-1).T), "keepm": keepm.reshape(D, N),
        "bdm": np.where(head[:, None] == head[None, :], scale, 0).astype(f32),
        "hm": np.where(head[:, None] == np.arange(HEADS)[None, :], scale, 0).astype(f32),
        "before": (step[:, None] < step[None, :]).astype(ml_dtypes.bfloat16),
        "all1": np.ones((T, T), ml_dtypes.bfloat16),
        "pick": (np.arange(128)[:, None] % E == np.arange(E * F)[None, :] // F).astype(np.float16),
    }
    nc = bacc.Bacc("TRN2", target_bir_lowering=False, num_devices=1)
    aps = {k: nc.dram_tensor(f"in_{k}", a.shape, mb.dt.from_np(a.dtype), kind="ExternalInput").ap()
           for k, a in arrays.items()}
    out = nc.dram_tensor("out", (D, SEQS * T), mb.dt.float32, kind="ExternalOutput").ap()
    audio_tower_kernel(nc, aps.pop("x"), aps, out)
    r = run(nc, [{f"in_{k}": a for k, a in arrays.items()}], core_ids=[0])
    return c(np.asarray(r.results[0]["out"]).reshape(D, SEQS, T).transpose(1, 2, 0))
```

```python
import concourse.bass as bass
from concourse import mybir
from contextlib import ExitStack

SEQS, T_IN, D = 128, 125, 128
T = T_IN + 1
GS = 4
GROUPS = SEQS // GS
N = GS * T
HEADS, KD = 8, 16
FC = 4
E, F = 64, 64
PAIRS = E // 2 + 1
SHARED = PAIRS - 1
TOP_K = 6
CAPACITY = SEQS * T * TOP_K * 2 // E
SHIFT = 10
HAND_OVER = 23
LAG = 2
BIG = 3.0e38

A_PE = ["zf_zi", "zh", "center", "var", "spread", "kv", "q", "g", "outer", "mix", "turn", "wo"]
A_ACT = ["zf", "zi", "zh", "abs", "exps", "sq", "c", "q", "g", "osq"]
A_DVE = ["mf", "mi", "mh", "n2", "d", "e", "m", "nd", "rd", "mr", "dm", "em",
         "ti", "tf", "pp", "pn", "a", "b", "den", "pd", "r1", "r2", "mv1", "mv2", "val", "s", "h1", "h2", "h3", "h",
         "ve", "src", "kv", "bd", "bds", "mu", "oc", "den1", "den2", "den3", "den4", "ovar", "ove", "on", "og", "r"]
A_POOL = ["rs", "ors0", "ors1", "ors2", "ors3"]
B_PE = ["var0", "spread0", "fc1_0", "fc1_1", "fc1_2", "fc1_3", "mean", "var1", "spread1", "fc2",
        "center2", "var2", "spread2", "center3", "var3", "spread3", "router", "rank", "turn"]
B_ACT = ["sq0", "hp0", "hp1", "hp2", "hp3", "gelu", "fsq0", "fsq1", "fsq2", "fsq3", "rsb",
         "sq2", "c2", "sq3", "c3", "xh", "exp"]
B_DVE = ["ve0", "t0", "x1", "hs0", "hs1", "hs2", "c_0", "c_1", "c_2", "c_3", "ve1", "r2a", "r2",
         "ve2", "y", "h1", "ve3", "xf", "lg", "top", "big", "match", "mask", "shift",
         "z", "em", "sum", "keep", "nrun", "tot", "inv", "gk", "gate", "gt_hi", "gt_lo"]
B_POOL = ["rs0", "sq01", "sq23", "sq0123", "rs1", "rs2", "rs3", "xl"]


def did(steps, step, g):
    return g * len(steps) + steps.index(step) + 1


def real(g):
    return 0 <= g < GROUPS if isinstance(g, int) else True


def is_number(g, n):
    return isinstance(g, int) and g == n


def from_group(g, n):
    return g >= n if isinstance(g, int) else True


def audio_tower_kernel(nc, x, w, out):
    fp32, f32r = mybir.dt.float32, mybir.dt.float32r
    bf16, fp16 = mybir.dt.bfloat16, mybir.dt.float16
    ALU, ACT = mybir.AluOpType, mybir.ActivationFunctionType
    AX = mybir.AxisListType.X

    ctx = ExitStack()
    with ctx:
        def sb(name, shape, dt=fp32):
            return ctx.enter_context(nc.sbuf_tensor(name, shape, dt))

        def bank(name):
            return ctx.enter_context(nc.psum_tensor(name, [128, 512], fp32))

        def sem(name):
            return ctx.enter_context(nc.semaphore(name))

        whi = sb("whi", [128, 3, PAIRS * 128], f32r)
        wlo = sb("wlo", [128, 3, PAIRS * 128], f32r)
        pick = sb("pick", [128, E * F], fp16)
        wtok = sb("wtok", [D, 3, D])
        wqgo = sb("wqgo", [D, 3, D])
        wkv = sb("wkv", [D, 2 * D])
        wfc1 = sb("wfc1", [D, FC * D])
        wfc2 = sb("wfc2", [D, FC, D])
        wrt = sb("wrt", [D, E])
        cmat = sb("cmat", [D, D])
        jmat = sb("jmat", [D, D])
        nth = sb("nth", [D, 2])
        ident = sb("ident", [T, T])
        dmt = sb("dmt", [T, HEADS, T])
        dsum = sb("dsum", [T, HEADS])
        bdm = sb("bdm", [D, D])
        hm = sb("hm", [D, HEADS])
        keepm = sb("keepm", [D, N])
        before = sb("before", [T, T], bf16)
        all1 = sb("all1", [T, T], bf16)
        ones = sb("ones", [T, 1])
        mhalf = sb("mhalf", [T, GS * HEADS])
        bkv = sb("bkv", [T, 2 * D])
        brt = sb("brt", [T, E])
        cols = sb("cols", [D, 11])
        bfc1 = sb("bfc1", [D, FC])
        lng = sb("lng", [D, FC])
        lnb = sb("lnb", [D, FC])
        bo_c = sb("bo_c", [D, 2])
        cb = sb("cb", [D, 1])
        col = {n: cols[:, i:i + 1] for i, n in enumerate(
            ["bf", "bi", "bh", "bq", "bg", "bo", "n0_g", "n0_b", "n1_g", "n1_b", "fc2_b"])}

        xin = sb("xin", [D, GS * T_IN])
        ar = sb("ar", [128, 8, 512])
        e_t = sb("e_t", [D, N])
        step_t = sb("step_t", [D, N])
        val_t = sb("val_t", [D, N])
        h0 = sb("h0", [D, N])
        bds = sb("bds", [D, GS * HEADS])
        a_small = sb("a_small", [T, 6, GS * HEADS])
        r_t = sb("r_t", [D, N])
        ff = sb("ff", [128, FC, 512])
        b_c = sb("b_c", [D, N])
        b_sq = sb("b_sq", [D, 2, N])
        b_x1 = sb("b_x1", [D, N])
        b_mix = sb("b_mix", [D, N])
        hb = sb("hb", [D, N])
        b_small = sb("b_small", [T, 8, 8])
        lg = sb("lg", [T, GS, E + 2])
        top = sb("top", [T, GS, 8])
        carrier = sb("carrier", [T, 2])
        nrun = sb("nrun", [T, E])
        mask = sb("mask", [T, GS, E], bf16)
        xh = sb("xh", [D, 2, N], f32r)
        xl = sb("xl", [D, 2, N], f32r)
        h1 = sb("h1", [D, 2, N])
        gt = sb("gt", [128, N], fp16)
        s_t = sb("s_t", [128, 2, N])
        t_t = sb("t_t", [128, N])
        h_t = sb("h_t", [128, 2, N])
        hh = sb("hh", [128, 2, N], f32r)
        hl = sb("hl", [128, 2, N], f32r)

        PG = [bank("PG0"), bank("PG1")]
        PU, PB, ACC = bank("PU"), bank("PB"), bank("ACC")
        FA = [bank("FA0"), bank("FA1")]
        FB = bank("FB")

        gru_consts_in, a_consts_in, b_consts_in = sem("gru_consts_in"), sem("a_consts_in"), sem("b_consts_in")
        chunk_in = [sem(f"chunk_in{i}") for i in range(FC)]
        setup_act, setup_dve, setup_pool, setup_pe = sem("setup_act"), sem("setup_dve"), sem("setup_pool"), sem("setup_pe")
        x_in, out_done = sem("x_in"), sem("out_done")
        a_pe, a_act, a_dve, a_pool = sem("a_pe"), sem("a_act"), sem("a_dve"), sem("a_pool")
        b_pe, b_act, b_dve, b_pool = sem("b_pe"), sem("b_act"), sem("b_dve"), sem("b_pool")
        hb_done = sem("hb_done")
        gate_done, up_done, spread_done, down_done = sem("gate_done"), sem("up_done"), sem("spread_done"), sem("down_done")
        silu_done, prod_done, h_done = sem("silu_done"), sem("prod_done"), sem("h_done")
        hh_done, hl_done, out_ready = sem("hh_done"), sem("hl_done"), sem("out_ready")

        block = ctx.enter_context(nc.Block())

        def seqs(t, lo=0):
            return t.rearrange("p (s t) -> p s t", t=T)[:, :, lo:T]

        tile = [ar[:, i, 0:N] for i in range(8)]
        zv = [FA[0][:, 0:GS * T_IN], FA[1][:, 0:GS * T_IN]]
        zs = [v.rearrange("p (s t) -> p s t", t=T_IN) for v in zv]
        body = lambda t: seqs(t, 1)
        kv = ar[0:T, 3:5, :].rearrange("p a (s c) -> p (a s) c", c=2 * D)
        bdv = ar[:, 5, :].rearrange("p (s c) -> p s c", c=D)
        oc = ar[0:T, 0, :]
        osq = ar[0:T, 1, :]
        heads = lambda t: t.rearrange("p (g k) -> p g k", k=KD)
        over_heads = lambda t: t.unsqueeze(2).to_broadcast([T, GS * HEADS, KD])
        ff_tile = [ff[:, j, 0:N] for j in range(FC)]
        square = [b_sq[:, 0, :], b_sq[:, 1, :], b_c[:, :], b_mix[:, :]]
        matched = ff[0:T, 0, 0:GS * (E + 2)].rearrange("p (s e) -> p s e", e=E + 2)
        ee = ff[0:T, 1, 0:GS * E].rearrange("p (s e) -> p s e", e=E)
        gk = ff[0:T, 2, 0:GS * E].rearrange("p (s e) -> p s e", e=E)
        g2 = ff[0:T, 3, :].rearrange("p (s e) -> p s e", e=2 * E)
        per_seq = lambda t: t.unsqueeze(2).to_broadcast([T, GS, E])
        router_out = FB[0:T, 0:GS * E].rearrange("p (s e) -> p s e", e=E)

        CHUNK = PAIRS * 128 // 11
        chunks = [(k, slice(c, c + CHUNK)) for c in range(0, PAIRS * 128, CHUNK) for k in range(3)]
        gru_loads = [
            (wtok[:, 0, :], w["wf"]), (wtok[:, 1, :], w["wi"]), (wtok[:, 2, :], w["wh"]),
            (cols[:, 0:1], w["bf"]), (cols[:, 1:2], w["bi"]), (cols[:, 2:3], w["bh"]),
            (keepm[:, :], w["keepm"]),
        ]
        a_loads = [
            (cmat[:, :], w["cmat"]), (nth[:, :], w["nth"]), (ident[:, :], w["ident"]),
            (wkv[:, 0:D], w["wk"]), (wkv[:, D:2 * D], w["wv"]),
            (bkv[:, 0:D], w["bk"].to_broadcast([T, D])), (bkv[:, D:2 * D], w["bv"].to_broadcast([T, D])),
            (wqgo[:, 0, :], w["wq"]), (wqgo[:, 1, :], w["wg"]), (wqgo[:, 2, :], w["wo"]),
            (cols[:, 3:4], w["bq"]), (cols[:, 4:5], w["bg"]), (cols[:, 5:6], w["bo"]),
            (dmt[:, :, :], w["dmt"]), (dsum[:, :], w["dsum"]), (bdm[:, :], w["bdm"]), (hm[:, :], w["hm"]),
        ]
        b_loads = [
            (cols[:, 6:7], w["n0_g"]), (cols[:, 7:8], w["n0_b"]), (cols[:, 8:9], w["n1_g"]), (cols[:, 9:10], w["n1_b"]),
            (cols[:, 10:11], w["fc2_b"]), (wfc1[:, :], w["fc1"]), (wfc2[:, :, :], w["fc2"]), (bfc1[:, :], w["fc1_b"]),
            (lng[:, :], w["lng"]), (lnb[:, :], w["lnb"]), (jmat[:, :], w["jmat"]), (wrt[:, :], w["router"]),
            (brt[:, :], w["rbias"].to_broadcast([T, E])), (before[:, :], w["before"]), (all1[:, :], w["all1"]),
            (pick[:, :], w["pick"]),
        ]
        GRU_CONSTS, A_CONSTS, B_CONSTS = 16 * len(gru_loads), 16 * len(a_loads), 16 * len(b_loads)
        MEMSETS = 7

        def pipeline(eng, one):
            for g in range(-3, 1):
                one(g, g % 2)
            with eng.Fori(0, GROUPS // 2 - 2) as pair_of_groups:
                one(pair_of_groups * 2 + 1, 1)
                one(pair_of_groups * 2 + 2, 0)
            for g in range(GROUPS - 3, GROUPS):
                one(g, g % 2)

        def a_part(p, g):
            return (p - SHIFT, g + 3) if p >= SHIFT else (p - SHIFT + PAIRS, g + 2)

        def chunk_at(p, g):
            n = (g + 3) * PAIRS + p - SHIFT - 1 if isinstance(g, int) else -1
            return n if 0 <= n < len(chunks) else None

        def pairs_before(g):
            return g * PAIRS

        def routed_before(g):
            return g * SHARED

        @block.sync
        def _(sp):
            sp.dma_start(xin[:, :], x[:, 0:GS, :].rearrange("p s t -> p (s t)")).then_inc(x_in, 16)
            for dst, src in gru_loads:
                sp.dma_start(dst, src).then_inc(gru_consts_in, 16)
            for dst, src in b_loads:
                sp.dma_start(dst, src).then_inc(b_consts_in, 16)
            for n, (k, cs) in enumerate(chunks):
                if n >= FC:
                    sp.wait_ge(setup_pool, n - FC + 1)
                sp.dma_start(ff[:, n % FC, 0:CHUNK], w["experts"][:, k, cs]).then_inc(chunk_in[n % FC], 16)

            def load_x(a):
                sp.wait_ge(a_pe, did(A_PE, "zh", a - 1))
                sp.dma_start(xin[:, :], x[:, bass.ds(a * GS, GS), :].rearrange("p s t -> p (s t)")).then_inc(x_in, 16)

            def store(g, par):
                sp.wait_ge(out_ready, g + 1)
                sp.dma_start(out[:, bass.ds(g * N, N)], h1[:, par, :]).then_inc(out_done, 16)

            def one(g, par):
                if real(g - 1):
                    store(g - 1, 1 - par)
                if real(g + 3) and from_group(g + 3, 1):
                    load_x(g + 3)
            pipeline(sp, one)
            store(GROUPS - 1, (GROUPS - 1) % 2)
            sp.wait_ge(out_done, 16 * GROUPS)

        @block.tensor
        def _(pe):
            mm = nc.tensor.matmul

            def one_pass(outp, lhs, rhs, start=True, stop=True):
                return mm(outp, lhs, rhs, start=start, stop=stop)

            def center(dst, src):
                return mm(dst[:, 0:N], cmat[:, :], src, start=True, stop=True)

            def variance(dst, sq, n, start=True, stop=True):
                for s in range(GS):
                    last = mm(dst[0:T, s:s + 1], sq[:, s * T:(s + 1) * T], nth[:, n:n + 1], start=start and s == 0,
                              stop=stop and s == GS - 1, skip_group_check=True)
                return last

            def spread(dst, rs):
                for s in range(GS):
                    last = mm(dst[:, s * T:(s + 1) * T], rs[:, s:s + 1].to_broadcast([T, 128]), ident[:, :],
                              start=True, stop=True, is_transpose=True)
                return last

            def stage_a(p, a):
                if p == 0:
                    pe.wait_ge(x_in, 16 * (a + 1))
                    if from_group(a, 1):
                        pe.wait_ge(a_dve, did(A_DVE, "r", a - 1))
                    mm(zv[0], wtok[:, 0, :], xin[:, :], start=True, stop=True)
                    mm(zv[1], wtok[:, 1, :], xin[:, :], start=True, stop=True).then_inc(a_pe, 1)
                if p == 1:
                    pe.wait_ge(a_act, did(A_ACT, "zf", a))
                    mm(zv[0], wtok[:, 2, :], xin[:, :], start=True, stop=True).then_inc(a_pe, 1)
                if p == 16:
                    pe.wait_ge(a_dve, did(A_DVE, "h", a))
                    pe.wait_ge(a_act, did(A_ACT, "zh", a))
                    if is_number(a, 0):
                        pe.wait_ge(a_consts_in, A_CONSTS)
                    center(FA[0], h0[:, :]).then_inc(a_pe, 1)
                if p == 17:
                    pe.wait_ge(a_act, did(A_ACT, "sq", a))
                    variance(FA[1], tile[1], 0).then_inc(a_pe, 1)
                if p == 20:
                    pe.wait_ge(a_pool, did(A_POOL, "rs", a))
                    pe.wait_ge(a_act, did(A_ACT, "c", a))
                    spread(FA[0], a_small[:, 1, 0:GS]).then_inc(a_pe, 1)
                if p == 22:
                    pe.wait_ge(a_dve, did(A_DVE, "src", a))
                    for s in range(GS):
                        last = mm(FA[s // 2][0:T, (s % 2) * 2 * D:(s % 2 + 1) * 2 * D], tile[2][:, s * T:(s + 1) * T],
                                  wkv[:, :], start=True, stop=True)
                    last.then_inc(a_pe, 1)
                for i, at in enumerate((23, 23)):
                    if p == at:
                        pe.wait_ge(a_dve, did(A_DVE, "kv", a))
                        mm(FA[i][:, 0:N], wqgo[:, i, :], tile[2], start=True, stop=True).then_inc(a_pe, 1)
                if p == 24:
                    pe.wait_ge(a_act, did(A_ACT, "g", a))
                    for s in range(GS):
                        mm(FA[0][:, s * D:(s + 1) * D], kv[:, s, 0:D], kv[:, s, D:2 * D], start=True, stop=True)
                    for s in range(GS):
                        last = mm(FA[1][:, s:s + 1], kv[:, s, 0:D], ones[:, :], start=True, stop=True)
                    last.then_inc(a_pe, 1)
                if p == 25:
                    pe.wait_ge(a_dve, did(A_DVE, "bds", a))
                    for s in range(GS):
                        mm(FA[0][0:T, s * D:(s + 1) * D], tile[6][:, s * T:(s + 1) * T], bdv[:, s, :],
                           start=s == 0, stop=False, skip_group_check=True)
                    for h in range(HEADS):
                        mm(FA[0][0:T, :].rearrange("p (s c) -> p s c", c=D)[:, :, h * KD:(h + 1) * KD], dmt[:, h, :],
                           kv[:, :, D + h * KD:D + (h + 1) * KD], start=False, stop=h == HEADS - 1, skip_group_check=True)
                    for s in range(GS):
                        last = mm(FA[1][0:T, s * HEADS:(s + 1) * HEADS], tile[6][:, s * T:(s + 1) * T],
                                  bds[:, s * HEADS:(s + 1) * HEADS], start=True, stop=True)
                    last.then_inc(a_pe, 1)
                if p == 31:
                    pe.wait_ge(a_dve, did(A_DVE, "on", a))
                    for s in range(GS):
                        last = nc.tensor.transpose(FA[0][:, s * T:(s + 1) * T], oc[:, s * D:(s + 1) * D], ident[:, :])
                    last.then_inc(a_pe, 1)
                if p == 32:
                    pe.wait_ge(a_dve, did(A_DVE, "og", a))
                    if is_number(a, 0):
                        pe.wait_ge(setup_dve, MEMSETS + 3)
                    mm(FA[1][:, 0:N], wqgo[:, 2, :], tile[1], start=True, stop=True).then_inc(a_pe, 1)

            def stage_b(p, b, par):
                if p == 1:
                    pe.wait_ge(b_act, did(B_ACT, "sq0", b))
                    if from_group(b, 1):
                        pe.wait_ge(b_dve, did(B_DVE, "gt_lo", b - 1))
                    variance(FB, b_sq[:, 0, :], 0).then_inc(b_pe, 1)
                if p == 2:
                    pe.wait_ge(b_pool, did(B_POOL, "rs0", b))
                    spread(FB, b_small[:, 1, 0:GS]).then_inc(b_pe, 1)
                for i, at in enumerate((3, 4, 5, 6)):
                    if p == at:
                        pe.wait_ge(b_dve, did(B_DVE, "x1", b))
                        if i:
                            pe.wait_ge(b_act, did(B_ACT, f"hp{i - 1}", b))
                        mm(FB[:, 0:N], wfc1[:, i * D:(i + 1) * D], b_x1[:, :], start=True, stop=True).then_inc(b_pe, 1)
                if p == 10:
                    pe.wait_ge(b_dve, did(B_DVE, "hs2", b))
                    mm(FB[:, 0:N], jmat[:, :], b_mix[:, :], start=True, stop=True).then_inc(b_pe, 1)
                if p == 14:
                    pe.wait_ge(b_pool, did(B_POOL, "sq0123", b))
                    pe.wait_ge(b_dve, did(B_DVE, "c_3", b))
                    variance(FB, b_sq[:, 0, :], 1).then_inc(b_pe, 1)
                if p == 15:
                    pe.wait_ge(b_pool, did(B_POOL, "rs1", b))
                    spread(FB, b_small[:, 3, 0:GS]).then_inc(b_pe, 1)
                for i, at in enumerate((16, 16, 16, 16)):
                    if p == at:
                        if i == 0:
                            pe.wait_ge(b_act, did(B_ACT, "rsb", b))
                        last = mm(FB[:, 0:N], wfc2[:, i, :], ff_tile[i], start=i == 0, stop=i == FC - 1)
                        if i == FC - 1:
                            last.then_inc(b_pe, 1)
                if p == 17:
                    pe.wait_ge(b_dve, did(B_DVE, "r2", b))
                    center(FB, b_mix[:, :]).then_inc(b_pe, 1)
                if p == 18:
                    pe.wait_ge(b_act, did(B_ACT, "c2", b))
                    variance(FB, b_sq[:, 0, :], 0).then_inc(b_pe, 1)
                if p == 19:
                    pe.wait_ge(b_pool, did(B_POOL, "rs2", b))
                    spread(FB, b_small[:, 5, 0:GS]).then_inc(b_pe, 1)
                if p == 20:
                    pe.wait_ge(b_dve, did(B_DVE, "h1", b))
                    center(FB, h1[:, par, :]).then_inc(b_pe, 1)
                if p == 21:
                    pe.wait_ge(b_act, did(B_ACT, "c3", b))
                    variance(FB, b_sq[:, 0, :], 0).then_inc(b_pe, 1)
                if p == 22:
                    pe.wait_ge(b_pool, did(B_POOL, "rs3", b))
                    spread(FB, b_small[:, 7, 0:GS]).then_inc(b_pe, 1)
                if p == 23:
                    pe.wait_ge(b_dve, did(B_DVE, "xf", b))
                    for s in range(GS):
                        last = mm(FB[0:T, s * E:(s + 1) * E], b_c[:, s * T:(s + 1) * T], wrt[:, :], start=True, stop=True)
                    last.then_inc(b_pe, 1)
                if p == 26:
                    pe.wait_ge(b_dve, did(B_DVE, "mask", b))
                    first = True
                    for s in range(GS + 1):
                        for earlier in range(s):
                            last = mm(FB[0:T, s * E:(s + 1) * E], all1[:, :], mask[:, earlier, :], start=first, stop=False,
                                      skip_group_check=True)
                            first = False
                        if s < GS:
                            last = mm(FB[0:T, s * E:(s + 1) * E], before[:, :], mask[:, s, :], start=first, stop=False,
                                      skip_group_check=True)
                            first = False
                    last.then_inc(b_pe, 1)
                if p == 31:
                    pe.wait_ge(b_dve, did(B_DVE, "gate", b))
                    for s in range(GS):
                        last = nc.tensor.transpose(FB[:, s * T:(s + 1) * T], g2[:, s, :], ident[:, :])
                    last.then_inc(b_pe, 1)

            def product(dst, kind, p, hi, lo, start, stop):
                cs = slice(p * 128, (p + 1) * 128)
                mm(dst[:, 0:N], whi[:, kind, cs], hi, start=start, stop=False)
                mm(dst[:, 0:N], wlo[:, kind, cs], hi, start=False, stop=False)
                return mm(dst[:, 0:N], whi[:, kind, cs], lo, start=False, stop=stop)

            def down(p, g, n, buf):
                pe.wait_ge(hl_done, n + 1)
                if p == 0 and from_group(g, 1):
                    pe.wait_ge(out_ready, g)
                product(ACC, 2, p, hh[:, buf, :], hl[:, buf, :], p == 0, p == SHARED).then_inc(down_done, 1)

            def fold_bias():
                pe.wait_ge(a_consts_in, A_CONSTS)
                mm(FB[:, 1:2], cmat[:, :], col["bo"], start=True, stop=True).then_inc(setup_pe, 1)
                pe.wait_ge(b_consts_in, B_CONSTS)
                for j in range(FC):
                    last = mm(FB[:, 0:1], wfc2[:, j, :], lnb[:, j:j + 1], start=j == 0, stop=j == FC - 1)
                last.then_inc(setup_pe, 1)

            def one(g, par):
                if is_number(g, -2):
                    fold_bias()
                if is_number(g, -1):
                    pe.wait_ge(setup_dve, MEMSETS + 5)
                if is_number(g, 0):
                    pe.wait_ge(setup_act, len(chunks))
                    pe.wait_ge(setup_pool, len(chunks))
                for p in range(PAIRS):
                    if real(g):
                        n = pairs_before(g) + p
                        b2 = (par + p) % 2
                        if p == 0:
                            pe.wait_ge(b_pool, did(B_POOL, "xl", g))
                        if from_group(g, 1) or p >= 2:
                            pe.wait_ge(silu_done, n - 1)
                        product(PG[b2], 0, p, xh[:, par, :], xl[:, par, :], True, True).then_inc(gate_done, 1)
                        if p >= 1:
                            pe.wait_ge(prod_done, routed_before(g) + p)
                        elif from_group(g, 1):
                            pe.wait_ge(h_done, n)
                        product(PU, 1, p, xh[:, par, :], xl[:, par, :], True, True).then_inc(up_done, 1)
                        if p != SHARED:
                            if p == 0:
                                pe.wait_ge(b_dve, did(B_DVE, "gt_lo", g))
                            if from_group(g, 1) or p >= 1:
                                pe.wait_ge(h_done, n)
                            mm(PB[:, 0:N], pick[:, p * 128:(p + 1) * 128], gt[:, :], start=True, stop=True)\
                                .then_inc(spread_done, 1)
                        if p >= LAG:
                            down(p - LAG, g, n - LAG, b2)
                        elif from_group(g, 1):
                            down(PAIRS + p - LAG, g - 1, n - LAG, b2)
                    if real(g + 1):
                        stage_b(p, g + 1, 1 - par)
                    q, a = a_part(p, g)
                    if real(a):
                        stage_a(q, a)

            pe.wait_ge(gru_consts_in, GRU_CONSTS)
            pe.wait_ge(setup_dve, MEMSETS)
            pipeline(pe, one)
            for p in range(PAIRS - LAG, PAIRS):
                n = (GROUPS - 1) * PAIRS + p
                down(p, GROUPS - 1, n, n % 2)

        @block.scalar
        def _(act):
            go = nc.scalar.activation

            def stage_a(p, early, a):
                if p == 0 and not early:
                    act.wait_ge(a_pe, did(A_PE, "zf_zi", a))
                    go(body(tile[0]), zs[0], ACT.Identity, bias=col["bf"]).then_inc(a_act, 1)
                    go(body(tile[1]), zs[1], ACT.Identity, bias=col["bi"]).then_inc(a_act, 1)
                if p == 1 and not early:
                    act.wait_ge(a_pe, did(A_PE, "zh", a))
                    go(body(tile[2]), zs[0], ACT.Identity, bias=col["bh"]).then_inc(a_act, 1)
                if p == 4 and not early:
                    act.wait_ge(a_dve, did(A_DVE, "mi", a))
                    go(body(tile[0]), body(tile[0]), ACT.Abs)
                    go(body(tile[1]), body(tile[1]), ACT.Abs).then_inc(a_act, 1)
                if p == 6 and not early:
                    act.wait_ge(a_act, did(A_ACT, "abs", a))
                    act.wait_ge(a_dve, did(A_DVE, "em", a))
                    for t, sign in ((tile[0], -1.0), (tile[1], -1.0), (tile[5], 1.0), (tile[4], 1.0), (step_t[:, :], 1.0),
                                    (tile[7], 1.0), (tile[3], -1.0), (tile[2], 1.0)):
                        last = go(body(t), body(t), ACT.Exp, scale=sign)
                    last.then_inc(a_act, 1)
                if p == 16 and not early:
                    if is_number(a, 0):
                        act.wait_ge(a_consts_in, A_CONSTS)
                    act.wait_ge(a_pe, did(A_PE, "center", a))
                    go(tile[1], FA[0][:, 0:N], ACT.Square).then_inc(a_act, 1)
                if p == 19 and not early:
                    go(tile[0], FA[0][:, 0:N], ACT.Copy).then_inc(a_act, 1)
                if p == 23 and not early:
                    act.wait_ge(a_pe, did(A_PE, "q", a))
                    go(tile[6], FA[0][:, 0:N], ACT.Identity, bias=col["bq"]).then_inc(a_act, 1)
                    act.wait_ge(a_pe, did(A_PE, "g", a))
                    go(tile[7], FA[1][:, 0:N], ACT.Silu, bias=col["bg"]).then_inc(a_act, 1)
                if p == 27 and early:
                    act.wait_ge(a_dve, did(A_DVE, "oc", a))
                    go(osq, oc, ACT.Square).then_inc(a_act, 1)

            def center_square(pe_step, b):
                act.wait_ge(b_pe, did(B_PE, pe_step, b))
                go(b_sq[:, 0, :], FB[:, 0:N], ACT.Square).then_inc(b_act, 1)
                go(b_c[:, :], FB[:, 0:N], ACT.Copy).then_inc(b_act, 1)

            def stage_b(p, early, b, par):
                if p == 0 and not early:
                    act.wait_ge(a_dve, did(A_DVE, "r", b))
                    if from_group(b, 1):
                        act.wait_ge(b_pe, did(B_PE, "var3", b - 1))
                    go(b_sq[:, 0, :], r_t[:, :], ACT.Square).then_inc(b_act, 1)
                for i, at in enumerate((4, 5, 6, 7)):
                    if p == at and early:
                        act.wait_ge(b_pe, did(B_PE, f"fc1_{i}", b))
                        go(ff_tile[i], FB[:, 0:N], ACT.Identity, bias=bfc1[:, i:i + 1]).then_inc(b_act, 1)
                if p == 8 and early:
                    act.wait_ge(b_act, did(B_ACT, "hp3", b))
                    for j in range(FC):
                        last = go(ff_tile[j], ff_tile[j], ACT.Gelu)
                    last.then_inc(b_act, 1)
                for i, at in enumerate((10, 10, 11, 11)):
                    if p == at and not early:
                        act.wait_ge(b_dve, did(B_DVE, f"c_{i}", b))
                        if i == FC - 1:
                            act.wait_ge(b_pe, did(B_PE, "mean", b))
                        go(square[i], ff_tile[i], ACT.Square).then_inc(b_act, 1)
                if p == 15 and not early:
                    act.wait_ge(b_pe, did(B_PE, "spread1", b))
                    act.wait_ge(b_pool, did(B_POOL, "sq23", b))
                    go(b_mix[:, :], FB[:, 0:N], ACT.Copy).then_inc(b_act, 1)
                if p == 17 and not early:
                    center_square("center2", b)
                if p == 20 and not early:
                    center_square("center3", b)
                if p == 23 and early:
                    act.wait_ge(b_dve, did(B_DVE, "xf", b))
                    if from_group(b, 2):
                        act.wait_ge(up_done, pairs_before(b - 1))
                    go(xh[:, par, :], b_c[:, :], ACT.Copy).then_inc(b_act, 1)
                if p == 26 and early:
                    act.wait_ge(b_dve, did(B_DVE, "shift", b))
                    go(ee, ee, ACT.Exp).then_inc(b_act, 1)

            def hand_over(a):
                act.wait_ge(a_dve, did(A_DVE, "h", a))
                if from_group(a, 1):
                    act.wait_ge(b_dve, did(B_DVE, "h1", a - 1))
                go(hb[:, :], h0[:, :], ACT.Identity, bias=col["n1_b"]).then_inc(hb_done, 1)

            def split_h(n, buf, has_down):
                act.wait_ge(h_done, n + 1)
                if has_down:
                    act.wait_ge(down_done, n - 1)
                go(hh[:, buf, :], h_t[:, buf, :], ACT.Copy).then_inc(hh_done, 1)

            def one(g, par):
                if is_number(g, -1):
                    act.wait_ge(b_consts_in, B_CONSTS)
                for p in range(PAIRS):
                    if real(g):
                        n = pairs_before(g) + p
                        b2 = (par + p) % 2
                        act.wait_ge(gate_done, n + 1)
                        if p == 1 and from_group(g, 1):
                            act.wait_ge(h_done, n - 1)
                        elif p != 1 and (from_group(g, 1) or p >= 2):
                            act.wait_ge(prod_done, routed_before(g) + p - 1)
                        go(s_t[:, b2, :], PG[b2][:, 0:N], ACT.Silu).then_inc(silu_done, 1)
                    q, a = a_part(p, g)
                    if real(g + 1):
                        stage_b(p, True, g + 1, 1 - par)
                    if real(a):
                        stage_a(q, True, a)
                    if real(g) and (from_group(g, 1) or p >= 1):
                        split_h(n - 1, 1 - b2, from_group(g, 1) or p >= 3)
                    if real(g + 1):
                        stage_b(p, False, g + 1, 1 - par)
                    if real(a):
                        stage_a(q, False, a)
                    if p == HAND_OVER and real(g + 2):
                        hand_over(g + 2)
                    n = chunk_at(p, g)
                    if n is not None:
                        k, cs = chunks[n]
                        act.wait_ge(chunk_in[n % FC], 16 * (n // FC + 1))
                        go(whi[:, k, cs], ff[:, n % FC, 0:CHUNK], ACT.Copy).then_inc(setup_act, 1)

            for dst, src in a_loads:
                act.dma_start(dst, src).then_inc(a_consts_in, 16)
            act.wait_ge(gru_consts_in, GRU_CONSTS)
            act.wait_ge(setup_dve, MEMSETS)
            pipeline(act, one)
            n = GROUPS * PAIRS - 1
            split_h(n, n % 2, True)

        @block.gpsimd
        def _(pool):
            def power(sem_done, dst, src, width):
                pool.tensor_tensor(dst, src, mhalf[:, 0:width], ALU.pow).then_inc(sem_done, 1)

            def stage_a(p, a):
                if p == 17:
                    pool.wait_ge(a_dve, did(A_DVE, "ve", a))
                    power(a_pool, a_small[:, 1, 0:GS], a_small[:, 0, 0:GS], GS)
                for i, at in enumerate((26, 27, 28, 28)):
                    if p == at:
                        pool.wait_ge(a_dve, did(A_DVE, "ove", a))
                        hs = slice(i * HEADS, (i + 1) * HEADS)
                        power(a_pool, a_small[:, 5, hs], a_small[:, 4, hs], HEADS)

            def stage_b(p, b, par):
                for i, at in enumerate((9, 10, 12)):
                    if p == at:
                        to, other = ((square[0], square[1]), (square[2], square[3]), (square[0], square[2]))[i]
                        pool.wait_ge(b_act, did(B_ACT, ("fsq1", "fsq3", "fsq3")[i], b))
                        if i == 2:
                            pool.wait_ge(b_pool, did(B_POOL, "sq23", b))
                        pool.tensor_tensor(to, to, other, ALU.add).then_inc(b_pool, 1)
                for i, at in enumerate((0, 13, 17, 20)):
                    if p == at:
                        pool.wait_ge(b_dve, did(B_DVE, f"ve{i}", b))
                        power(b_pool, b_small[:, 2 * i + 1, 0:GS], b_small[:, 2 * i, 0:GS], GS)
                if p == 24:
                    pool.wait_ge(b_act, did(B_ACT, "xh", b))
                    pool.tensor_tensor(xl[:, par, :], b_c[:, :], xh[:, par, :].bitcast(fp32), ALU.subtract)\
                        .then_inc(b_pool, 1)

            def one(g, par):
                for p in range(PAIRS):
                    if real(g):
                        n = pairs_before(g) + p
                        b2 = (par + p) % 2
                        pool.wait_ge(hh_done, n + 1)
                        if from_group(g, 1) or p >= 2:
                            pool.wait_ge(down_done, n - 1)
                        pool.tensor_tensor(hl[:, b2, :], h_t[:, b2, :], hh[:, b2, :].bitcast(fp32), ALU.subtract)\
                            .then_inc(hl_done, 1)
                    if real(g + 1):
                        stage_b(p, g + 1, 1 - par)
                    q, a = a_part(p, g)
                    if real(a):
                        stage_a(q, a)

                    n = chunk_at(p, g)
                    if n is not None:
                        k, cs = chunks[n]
                        pool.wait_ge(setup_act, n + 1)
                        pool.tensor_tensor(wlo[:, k, cs], ff[:, n % FC, 0:CHUNK], whi[:, k, cs].bitcast(fp32),
                                           ALU.subtract).then_inc(setup_pool, 1)

            pool.wait_ge(setup_dve, MEMSETS)
            pipeline(pool, one)

        @block.vector
        def _(dve):
            tt, ts, stt = dve.tensor_tensor, dve.tensor_scalar, dve.scalar_tensor_tensor
            add, sub, mul = ALU.add, ALU.subtract, ALU.mult

            def stage_a(p, a):
                def after(step):
                    dve.wait_ge(a_dve, did(A_DVE, step, a))
                B = [body(t) for t in tile]
                if p == 0:
                    dve.wait_ge(a_act, did(A_ACT, "zf", a))
                    ts(B[3], B[0], 0.0, None, ALU.min).then_inc(a_dve, 1)
                if p == 1:
                    dve.wait_ge(a_act, did(A_ACT, "zi", a))
                    ts(B[4], B[1], 0.0, None, ALU.min).then_inc(a_dve, 1)
                    dve.wait_ge(a_act, did(A_ACT, "zh", a))
                    ts(B[5], B[2], 0.0, None, ALU.min).then_inc(a_dve, 1)
                    ts(B[6], B[2], 0.0, 2.0, ALU.max, mul).then_inc(a_dve, 1)
                if p == 2:
                    after("mi")
                    tt(B[3], B[4], B[3], sub).then_inc(a_dve, 1)
                    after("d")
                    tt(body(e_t[:, :]), B[3], B[5], add).then_inc(a_dve, 1)
                if p == 3:
                    after("e")
                    dve.tensor_tensor_scan(tile[4], keepm[:, :], e_t[:, :], 0.0, mul, ALU.max).then_inc(a_dve, 1)
                    after("n2")
                    ts(B[2], B[3], 0.0, None, ALU.min).then_inc(a_dve, 1)
                    after("nd")
                    ts(B[3], B[3], 0.0, None, ALU.max).then_inc(a_dve, 1)
                if p == 4:
                    after("rd")
                    tt(B[7], B[4], B[3], sub).then_inc(a_dve, 1)
                if p == 5:
                    tt(body(step_t[:, :]), seqs(tile[4])[:, :, 0:T_IN], B[4], sub).then_inc(a_dve, 1)
                    after("dm")
                    tt(B[4], body(e_t[:, :]), B[4], sub).then_inc(a_dve, 1)
                if p == 6:
                    dve.wait_ge(a_act, did(A_ACT, "exps", a))
                    ts(B[1], B[1], 1.0, None, add).then_inc(a_dve, 1)
                    ts(B[0], B[0], 1.0, None, add).then_inc(a_dve, 1)
                    after("ti")
                    stt(B[5], B[5], 1.0, B[1], add, mul).then_inc(a_dve, 1)
                    after("tf")
                    stt(B[6], B[6], 1.0, B[0], add, mul).then_inc(a_dve, 1)
                if p == 7:
                    tt(B[3], B[3], B[1], mul).then_inc(a_dve, 1)
                    tt(B[2], B[2], B[0], mul).then_inc(a_dve, 1)
                if p == 8:
                    after("b")
                    tt(B[3], B[3], B[2], add).then_inc(a_dve, 1)
                    after("den")
                    tt(B[2], B[3], B[5], mul).then_inc(a_dve, 1)
                for i, at in enumerate((10, 10)):
                    if p == at:
                        after("pd")
                        half = B[2][:, 2 * i:2 * i + 2, :]
                        dve.reciprocal(half, half).then_inc(a_dve, 1)
                if p == 11:
                    after("r2")
                    tt(B[6], B[6], B[2], mul).then_inc(a_dve, 1)
                    after("mv1")
                    tt(B[6], B[6], B[3], mul).then_inc(a_dve, 1)
                    after("mv2")
                    tt(body(val_t[:, :]), B[6], B[4], mul).then_inc(a_dve, 1)
                if p == 12:
                    after("val")
                    dve.tensor_tensor_scan(tile[0], step_t[:, :], val_t[:, :], 0.0, mul, add).then_inc(a_dve, 1)
                if p == 13:
                    after("s")
                    tt(B[7], B[7], B[0], mul).then_inc(a_dve, 1)
                if p == 14:
                    after("h1")
                    tt(B[7], B[7], B[1], mul).then_inc(a_dve, 1)
                if p == 15:
                    after("h2")
                    tt(B[7], B[7], B[2], mul).then_inc(a_dve, 1)
                    after("h3")
                    if from_group(a, 1):
                        dve.wait_ge(hb_done, a)
                    tt(body(h0[:, :]), B[7], B[5], mul).then_inc(a_dve, 1)
                if p == 18:
                    if is_number(a, 0):
                        dve.wait_ge(a_consts_in, A_CONSTS)
                    dve.wait_ge(a_pe, did(A_PE, "var", a))
                    ts(a_small[:, 0, 0:GS], FA[1][0:T, 0:GS], 1e-5, None, add).then_inc(a_dve, 1)
                if p == 20:
                    dve.wait_ge(a_pe, did(A_PE, "spread", a))
                    tt(tile[2], tile[0], FA[0][:, 0:N], mul).then_inc(a_dve, 1)
                if p == 22:
                    dve.wait_ge(a_pe, did(A_PE, "kv", a))
                    bias2 = bkv[:, :].unsqueeze(1).to_broadcast([T, 2, 2 * D])
                    for i in (0, 1):
                        last = tt(kv[:, 2 * i:2 * i + 2, :], FA[i][0:T, :].rearrange("p (s c) -> p s c", c=2 * D), bias2, add)
                    last.then_inc(a_dve, 1)
                if p == 24:
                    dve.wait_ge(a_pe, did(A_PE, "outer", a))
                    tt(bdv, FA[0][:, :].rearrange("p (s c) -> p s c", c=D),
                       bdm[:, :].unsqueeze(1).to_broadcast([D, GS, D]), mul).then_inc(a_dve, 1)
                    tt(bds[:, :].rearrange("p (s h) -> p s h", h=HEADS), FA[1][:, 0:GS].unsqueeze(2).to_broadcast([D, GS, HEADS]),
                       hm[:, :].unsqueeze(1).to_broadcast([D, GS, HEADS]), mul).then_inc(a_dve, 1)
                if p == 25:
                    dve.wait_ge(a_pe, did(A_PE, "mix", a))
                    dve.tensor_reduce(a_small[:, 2, :], heads(FA[0][0:T, :]), AX, add).then_inc(a_dve, 1)
                    after("mu")
                    stt(heads(oc), over_heads(a_small[:, 2, :]), -1.0 / KD, heads(FA[0][0:T, :]), mul, add).then_inc(a_dve, 1)
                if p == 25:
                    tt(a_small[:, 3, :].rearrange("p (s h) -> p s h", h=HEADS),
                       FA[1][0:T, 0:GS * HEADS].rearrange("p (s h) -> p s h", h=HEADS),
                       dsum[:, :].unsqueeze(1).to_broadcast([T, GS, HEADS]), add).then_inc(a_dve, 1)
                    after("den1")
                    stt(a_small[:, 3, :], a_small[:, 3, :], -1.0, a_small[:, 3, :], mul, ALU.max).then_inc(a_dve, 1)
                if p == 26:
                    after("den2")
                    ts(a_small[:, 3, :], a_small[:, 3, :], 1.0, None, ALU.max).then_inc(a_dve, 1)
                    after("den3")
                    stt(a_small[:, 3, :], a_small[:, 3, :], 1e-6, a_small[:, 3, :], mul, mul).then_inc(a_dve, 1)
                if p == 27:
                    dve.wait_ge(a_act, did(A_ACT, "osq", a))
                    dve.tensor_reduce(a_small[:, 2, :], heads(osq), AX, add).then_inc(a_dve, 1)
                    after("ovar")
                    stt(a_small[:, 4, :], a_small[:, 2, :], 1.0 / KD, a_small[:, 3, :], mul, add).then_inc(a_dve, 1)
                if p == 30:
                    dve.wait_ge(a_pool, did(A_POOL, "ors3", a))
                    tt(heads(oc), heads(oc), over_heads(a_small[:, 5, :]), mul).then_inc(a_dve, 1)
                if p == 31:
                    dve.wait_ge(a_pe, did(A_PE, "turn", a))
                    tt(tile[1], tile[7], FA[0][:, 0:N], mul).then_inc(a_dve, 1)
                if p == 32:
                    dve.wait_ge(a_pe, did(A_PE, "wo", a))
                    if from_group(a, 1):
                        dve.wait_ge(b_dve, did(B_DVE, "t0", a - 1))
                    stt(r_t[:, :], FA[1][:, 0:N], bo_c[:, 0:1], tile[2], add, add).then_inc(a_dve, 1)

            def stage_b(p, b, par):
                def after(step):
                    dve.wait_ge(b_dve, did(B_DVE, step, b))

                def var_eps(i, pe_step, eps):
                    dve.wait_ge(b_pe, did(B_PE, pe_step, b))
                    ts(b_small[:, 2 * i, 0:GS], FB[0:T, 0:GS], eps, None, add).then_inc(b_dve, 1)
                if p == 1:
                    var_eps(0, "var0", 1e-5)
                if p == 2:
                    dve.wait_ge(b_pe, did(B_PE, "spread0", b))
                    tt(b_x1[:, :], r_t[:, :], FB[:, 0:N], mul).then_inc(b_dve, 1)
                    after("t0")
                    ts(b_x1[:, :], b_x1[:, :], col["n0_g"], col["n0_b"], mul, add).then_inc(b_dve, 1)
                if p == 8:
                    dve.wait_ge(b_act, did(B_ACT, "gelu", b))
                    tt(b_mix[:, :], ff_tile[0], ff_tile[1], add).then_inc(b_dve, 1)
                    after("hs0")
                    tt(b_mix[:, :], b_mix[:, :], ff_tile[2], add).then_inc(b_dve, 1)
                if p == 9:
                    after("hs1")
                    tt(b_mix[:, :], b_mix[:, :], ff_tile[3], add).then_inc(b_dve, 1)
                for i, at in enumerate((10, 10, 10, 10)):
                    if p == at:
                        dve.wait_ge(b_pe, did(B_PE, "mean", b))
                        tt(ff_tile[i], ff_tile[i], FB[:, 0:N], sub).then_inc(b_dve, 1)
                if p == 14:
                    var_eps(1, "var1", 1e-6)
                if p == 16:
                    dve.wait_ge(b_pe, did(B_PE, "fc2", b))
                    tt(b_mix[:, :], b_mix[:, :], FB[:, 0:N], mul).then_inc(b_dve, 1)
                    after("r2a")
                    stt(b_mix[:, :], b_mix[:, :], cb[:, :], b_x1[:, :], add, add).then_inc(b_dve, 1)
                if p == 18:
                    var_eps(2, "var2", 1e-5)
                if p == 19:
                    dve.wait_ge(b_pe, did(B_PE, "spread2", b))
                    tt(b_x1[:, :], b_c[:, :], FB[:, 0:N], mul).then_inc(b_dve, 1)
                    after("y")
                    dve.wait_ge(hb_done, b + 1)
                    if from_group(b, 2):
                        dve.wait_ge(out_done, 16 * (b - 1))
                    stt(h1[:, par, :], b_x1[:, :], col["n1_g"], hb[:, :], mul, add).then_inc(b_dve, 1)
                if p == 21:
                    var_eps(3, "var3", 1e-5)
                if p == 22:
                    dve.wait_ge(b_pe, did(B_PE, "spread3", b))
                    tt(b_c[:, :], b_c[:, :], FB[:, 0:N], mul).then_inc(b_dve, 1)
                if p == 23:
                    dve.wait_ge(b_pe, did(B_PE, "router", b))
                    tt(lg[:, :, 0:E], router_out, brt[:, :].unsqueeze(1).to_broadcast([T, GS, E]), add).then_inc(b_dve, 1)
                    after("lg")
                    dve.memset(carrier[:, 0:1], 0.0)
                    for s in range(GS):
                        last = dve.max(top[:, s, :], lg[:, s, 0:E])
                    last.then_inc(b_dve, 1)
                if p == 24:
                    after("top")
                    dve.memset(top[:, :, TOP_K:8], BIG).then_inc(b_dve, 1)
                if p == 24:
                    after("big")
                    dve.memset(carrier[:, 1:2], 0.0)
                    for s in range(GS):
                        last = dve.match_replace(matched[:, s, :], top[:, s, :], lg[:, s, :], -BIG)
                    last.then_inc(b_dve, 1)
                if p == 25:
                    after("match")
                    tt(mask[:, :, :], matched[:, :, 0:E], lg[:, :, 0:E], ALU.not_equal).then_inc(b_dve, 1)
                    tt(ee, lg[:, :, 0:E], per_seq(top[:, :, 0]), sub).then_inc(b_dve, 1)
                if p == 26:
                    dve.wait_ge(b_act, did(B_ACT, "exp", b))
                    dve.tensor_reduce(b_small[:, 0, 4:8], ee, AX, add).then_inc(b_dve, 1)
                    tt(gk, ee, mask[:, :, :], mul).then_inc(b_dve, 1)
                    after("em")
                    dve.tensor_reduce(b_small[:, 1, 4:8], gk, AX, add).then_inc(b_dve, 1)
                if p == 26:
                    dve.wait_ge(b_pe, did(B_PE, "rank", b))
                    stt(ee, router_out, float(CAPACITY), nrun[:, :].unsqueeze(1).to_broadcast([T, GS, E]), sub, ALU.is_lt)\
                        .then_inc(b_dve, 1)
                    after("keep")
                    tt(nrun[:, :], nrun[:, :], FB[0:T, GS * E:(GS + 1) * E], sub).then_inc(b_dve, 1)
                    after("sum")
                    stt(b_small[:, 2, 4:8], b_small[:, 0, 4:8], 1e-9, b_small[:, 1, 4:8], mul, add).then_inc(b_dve, 1)
                    after("tot")
                    dve.reciprocal(b_small[:, 3, 4:8], b_small[:, 2, 4:8]).then_inc(b_dve, 1)
                    tt(gk, gk, ee, mul).then_inc(b_dve, 1)
                if p == 30:
                    after("gk")
                    for half in (0, 1):
                        last = tt(g2[:, :, half * E:(half + 1) * E], gk, per_seq(b_small[:, 3, 4:8]), mul)
                    last.then_inc(b_dve, 1)
                if p == 31:
                    dve.wait_ge(b_pe, did(B_PE, "turn", b))
                    if from_group(b, 1):
                        dve.wait_ge(spread_done, b * SHARED)
                    dve.tensor_copy(gt[:, :], FB[:, 0:N]).then_inc(b_dve, 1)
                    after("gt_hi")
                    tt(gt[E:2 * E, :], FB[E:2 * E, 0:N], gt[E:2 * E, :], sub).then_inc(b_dve, 1)

            def finish(g, par):
                dve.wait_ge(down_done, pairs_before(g + 1))
                tt(h1[:, par, :], h1[:, par, :], ACC[:, 0:N], add).then_inc(out_ready, 1)

            def center_wo():
                dve.wait_ge(a_consts_in, A_CONSTS)
                dve.tensor_reduce(bo_c[:, 1:2], wqgo[:, 2, :], AX, add).then_inc(setup_dve, 1)
                dve.wait_ge(setup_dve, MEMSETS + 1)
                ts(bo_c[:, 1:2], bo_c[:, 1:2], 1.0 / D, None, mul).then_inc(setup_dve, 1)
                dve.wait_ge(setup_pe, 2)
                dve.tensor_copy(bo_c[:, 0:1], FB[:, 1:2])
                dve.wait_ge(setup_dve, MEMSETS + 2)
                ts(wqgo[:, 2, :], wqgo[:, 2, :], bo_c[:, 1:2], None, sub).then_inc(setup_dve, 1)

            def fold_gain():
                dve.wait_ge(b_consts_in, B_CONSTS)
                dve.wait_ge(setup_pe, 2)
                for j in range(FC):
                    last = ts(wfc2[:, j, :], wfc2[:, j, :], lng[:, j:j + 1], None, mul)
                last.then_inc(setup_dve, 1)
                tt(cb[:, :], FB[:, 0:1], col["fc2_b"], add).then_inc(setup_dve, 1)

            def one(g, par):
                if is_number(g, -2):
                    center_wo()
                    dve.wait_ge(setup_dve, MEMSETS + 3)
                if is_number(g, -1):
                    fold_gain()
                    dve.wait_ge(setup_dve, MEMSETS + 5)
                for p in range(PAIRS):
                    if real(g):
                        n = pairs_before(g) + p
                        b2 = (par + p) % 2
                        dve.wait_ge(silu_done, n + 1)
                        dve.wait_ge(up_done, n + 1)
                        if p != SHARED:
                            if from_group(g, 1) or p >= 1:
                                dve.wait_ge(h_done, n)
                            tt(t_t[:, :], s_t[:, b2, :], PU[:, 0:N], mul).then_inc(prod_done, 1)
                            dve.wait_ge(prod_done, routed_before(g) + p + 1)
                            dve.wait_ge(spread_done, routed_before(g) + p + 1)
                            if from_group(g, 1) or p >= 2:
                                dve.wait_ge(hl_done, n - 1)
                            tt(h_t[:, b2, :], t_t[:, :], PB[:, 0:N], mul).then_inc(h_done, 1)
                        else:
                            dve.wait_ge(hl_done, n - 1)
                            stt(h_t[:, b2, :], s_t[:, b2, :], 0.5, PU[:, 0:N], mul, mul).then_inc(h_done, 1)
                        if p == LAG - 1 and from_group(g, 1):
                            finish(g - 1, 1 - par)
                    if real(g + 1):
                        stage_b(p, g + 1, 1 - par)
                    q, a = a_part(p, g)
                    if real(a):
                        stage_a(q, a)

            dve.memset(e_t[:, :], 0.0)
            dve.memset(step_t[:, :], 0.0)
            dve.memset(val_t[:, :], 0.5)
            dve.memset(h0[:, :], 0.5).then_inc(setup_dve, 4)
            dve.memset(ones[:, :], 1.0)
            dve.memset(mhalf[:, :], -0.5)
            dve.memset(nrun[:, :], 0.0)
            dve.memset(lg[:, :, E:E + 2], BIG).then_inc(setup_dve, 3)
            dve.wait_ge(setup_dve, MEMSETS)
            dve.wait_ge(gru_consts_in, GRU_CONSTS)
            pipeline(dve, one)
            finish(GROUPS - 1, (GROUPS - 1) % 2)


def kernel(**inputs):
    import numpy as np
    import concourse.bacc as bacc
    from concourse import mybir as mb
    from concourse.bass_utils import run_bass_kernel_spmd as run

    def c(a):
        return np.ascontiguousarray(a)

    i = {k: np.asarray(v) for k, v in inputs.items()}
    column = lambda a: c(a.reshape(-1, 1))
    f32 = np.float32
    experts = np.empty((128, 3, PAIRS * 128), f32)
    for kind, (routed, shared) in enumerate((("w_gate", "shared_w_gate"), ("w_up", "shared_w_up"))):
        experts[:, kind, :E * F] = i["L0_ffn_" + routed].reshape(E * F, D).T
        experts[:, kind, E * F:] = i["L0_ffn_" + shared].reshape(2 * F, D).T
    for lo, a in ((0, i["L0_ffn_w_down"]), (SHARED, i["L0_ffn_shared_w_down"])):
        n = a.shape[0] // 2
        experts[:, 2, lo * 128:(lo + n) * 128] = a.reshape(n, 2, D, F).transpose(1, 3, 0, 2).reshape(128, n * D)

    step = np.arange(T)
    diff = (step[:, None] - step[None, :]).astype(f32)
    decay = np.log(f32(1) - f32(2) ** (f32(-5) - np.arange(HEADS, dtype=f32))).astype(f32)
    dm = np.where(diff[None] >= 0, np.exp(diff[None] * decay[:, None, None]), 0).astype(f32)
    dm = dm / np.sqrt(dm.sum(-1, keepdims=True))
    head = np.arange(D) // KD
    keepm = np.ones((D, GS, T), f32)
    keepm[:, :, 0] = 0
    scale = KD ** -0.5
    import ml_dtypes
    arrays = {
        "x": c(i["x"].transpose(2, 0, 1)),
        "experts": experts,
        "wf": c(i["L0_tok_Wf"]), "wi": c(i["L0_tok_Wi"]), "wh": c(i["L0_tok_Wh"]),
        "bf": column(i["L0_tok_bf"]), "bi": column(i["L0_tok_bi"]), "bh": column(i["L0_tok_bh"]),
        "wq": c(i["L0_attn_wq"].T), "wg": c(i["L0_attn_wg"].T), "wo": c(i["L0_attn_wo"].T),
        "wk": c(i["L0_attn_wk"].T), "wv": c(i["L0_attn_wv"].T),
        "bq": column(i["L0_attn_bq"]), "bg": column(i["L0_attn_bg"]), "bo": column(i["L0_attn_bo"]),
        "bk": i["L0_attn_bk"].reshape(1, D), "bv": i["L0_attn_bv"].reshape(1, D),
        "n0_g": column(i["L0_attn_n0_g"]), "n0_b": column(i["L0_attn_n0_b"]),
        "n1_g": column(i["L0_attn_n1_g"]), "n1_b": column(i["L0_attn_n1_b"]),
        "fc1": c(i["L0_attn_fc1_w"].T), "fc1_b": c(i["L0_attn_fc1_b"].reshape(FC, D).T),
        "fc2": c(i["L0_attn_fc2_w"].reshape(D, FC, D).transpose(2, 1, 0)), "fc2_b": column(i["L0_attn_fc2_b"]),
        "lng": c(i["L0_attn_ln_ffn_g"].reshape(FC, D).T), "lnb": c(i["L0_attn_ln_ffn_b"].reshape(FC, D).T),
        "router": c(i["L0_ffn_router_w"].T), "rbias": i["L0_ffn_bias"].reshape(1, E),
        "cmat": (np.eye(D) - 1.0 / D).astype(f32), "jmat": np.full((D, D), 1.0 / (FC * D), f32),
        "nth": np.tile(np.array([[1.0 / D, 1.0 / (FC * D)]], f32), (D, 1)), "ident": np.eye(T, dtype=f32),
        "dmt": c(dm.transpose(2, 0, 1)), "dsum": c(dm.sum(-1).T), "keepm": keepm.reshape(D, N),
        "bdm": np.where(head[:, None] == head[None, :], scale, 0).astype(f32),
        "hm": np.where(head[:, None] == np.arange(HEADS)[None, :], scale, 0).astype(f32),
        "before": (step[:, None] < step[None, :]).astype(ml_dtypes.bfloat16),
        "all1": np.ones((T, T), ml_dtypes.bfloat16),
        "pick": (np.arange(128)[:, None] % E == np.arange(E * F)[None, :] // F).astype(np.float16),
    }
    nc = bacc.Bacc("TRN2", target_bir_lowering=False, num_devices=1)
    aps = {k: nc.dram_tensor(f"in_{k}", a.shape, mb.dt.from_np(a.dtype), kind="ExternalInput").ap()
           for k, a in arrays.items()}
    out = nc.dram_tensor("out", (D, SEQS * T), mb.dt.float32, kind="ExternalOutput").ap()
    audio_tower_kernel(nc, aps.pop("x"), aps, out)
    r = run(nc, [{f"in_{k}": a for k, a in arrays.items()}], core_ids=[0])
    return c(np.asarray(r.results[0]["out"]).reshape(D, SEQS, T).transpose(1, 2, 0))
```
